# Optimizing a Trainium2 kernel written in Bass

```python
import numpy as np
import jax
import jax.numpy as jnp

def _softmax(x, axis=-1):
    return jax.nn.softmax(x, axis=axis)

def _gelu(x):
    return jax.nn.gelu(x, approximate=True)

def _silu(x):
    return jax.nn.silu(x)

def _sigmoid(x):
    return jax.nn.sigmoid(x)

def _layernorm(x, axis=-1, eps=1e-05):
    m = jnp.mean(x, axis=axis, keepdims=True)
    v = jnp.var(x, axis=axis, keepdims=True)
    return (x - m) / jnp.sqrt(v + eps)

def _scatter_add(tgt, idx, src, axis=0):
    return tgt.at[idx].add(src)

def _segment_sum(src, seg, n):
    return jax.ops.segment_sum(src, seg, n)
kernel_name = 'mk_dlrm_tower_d1_rec_r8_b570c2'

def setup_inputs(seed: int=0):
    np.random.seed(seed)
    _w = jnp.asarray

    def _rec_inputs():
        import jax
        import jax.numpy as jnp
        _tk = jax.random.key(seed)
        dense_ctx = jax.random.normal(jax.random.fold_in(_tk, 190), (1024, 16), jnp.float32)
        ids = jnp.stack([jax.random.randint(jax.random.fold_in(_tk, 200 + f), (1024,), 0, v, jnp.int32) for f, v in enumerate([125000, 125000, 1000, 125000, 1250, 125000, 125000, 12500, 1000, 12500, 12500, 1000, 125000, 12500, 125000, 125000, 125000, 1250, 1250, 1000, 125000, 1250, 1000, 1250, 1250, 125000, 12500, 12500, 1250, 125000, 125000, 125000, 1000, 1250, 12500, 1000, 1000, 1000, 1000, 1000])], axis=1)
        tbl_0 = 0.05 * jax.random.normal(jax.random.fold_in(_tk, 500 + 0), (125000, 16), jnp.float32)
        tbl_1 = 0.05 * jax.random.normal(jax.random.fold_in(_tk, 500 + 1), (125000, 16), jnp.float32)
        tbl_2 = 0.05 * jax.random.normal(jax.random.fold_in(_tk, 500 + 2), (1000, 16), jnp.float32)
        tbl_3 = 0.05 * jax.random.normal(jax.random.fold_in(_tk, 500 + 3), (125000, 16), jnp.float32)
        tbl_4 = 0.05 * jax.random.normal(jax.random.fold_in(_tk, 500 + 4), (1250, 16), jnp.float32)
        tbl_5 = 0.05 * jax.random.normal(jax.random.fold_in(_tk, 500 + 5), (125000, 16), jnp.float32)
        tbl_6 = 0.05 * jax.random.normal(jax.random.fold_in(_tk, 500 + 6), (125000, 16), jnp.float32)
        tbl_7 = 0.05 * jax.random.normal(jax.random.fold_in(_tk, 500 + 7), (12500, 16), jnp.float32)
        tbl_8 = 0.05 * jax.random.normal(jax.random.fold_in(_tk, 500 + 8), (1000, 16), jnp.float32)
        tbl_9 = 0.05 * jax.random.normal(jax.random.fold_in(_tk, 500 + 9), (12500, 16), jnp.float32)
        tbl_10 = 0.05 * jax.random.normal(jax.random.fold_in(_tk, 500 + 10), (12500, 16), jnp.float32)
        tbl_11 = 0.05 * jax.random.normal(jax.random.fold_in(_tk, 500 + 11), (1000, 16), jnp.float32)
        tbl_12 = 0.05 * jax.random.normal(jax.random.fold_in(_tk, 500 + 12), (125000, 16), jnp.float32)
        tbl_13 = 0.05 * jax.random.normal(jax.random.fold_in(_tk, 500 + 13), (12500, 16), jnp.float32)
        tbl_14 = 0.05 * jax.random.normal(jax.random.fold_in(_tk, 500 + 14), (125000, 16), jnp.float32)
        tbl_15 = 0.05 * jax.random.normal(jax.random.fold_in(_tk, 500 + 15), (125000, 16), jnp.float32)
        tbl_16 = 0.05 * jax.random.normal(jax.random.fold_in(_tk, 500 + 16), (125000, 16), jnp.float32)
        tbl_17 = 0.05 * jax.random.normal(jax.random.fold_in(_tk, 500 + 17), (1250, 16), jnp.float32)
        tbl_18 = 0.05 * jax.random.normal(jax.random.fold_in(_tk, 500 + 18), (1250, 16), jnp.float32)
        tbl_19 = 0.05 * jax.random.normal(jax.random.fold_in(_tk, 500 + 19), (1000, 16), jnp.float32)
        tbl_20 = 0.05 * jax.random.normal(jax.random.fold_in(_tk, 500 + 20), (125000, 16), jnp.float32)
        tbl_21 = 0.05 * jax.random.normal(jax.random.fold_in(_tk, 500 + 21), (1250, 16), jnp.float32)
        tbl_22 = 0.05 * jax.random.normal(jax.random.fold_in(_tk, 500 + 22), (1000, 16), jnp.float32)
        tbl_23 = 0.05 * jax.random.normal(jax.random.fold_in(_tk, 500 + 23), (1250, 16), jnp.float32)
        tbl_24 = 0.05 * jax.random.normal(jax.random.fold_in(_tk, 500 + 24), (1250, 16), jnp.float32)
        tbl_25 = 0.05 * jax.random.normal(jax.random.fold_in(_tk, 500 + 25), (125000, 16), jnp.float32)
        tbl_26 = 0.05 * jax.random.normal(jax.random.fold_in(_tk, 500 + 26), (12500, 16), jnp.float32)
        tbl_27 = 0.05 * jax.random.normal(jax.random.fold_in(_tk, 500 + 27), (12500, 16), jnp.float32)
        tbl_28 = 0.05 * jax.random.normal(jax.random.fold_in(_tk, 500 + 28), (1250, 16), jnp.float32)
        tbl_29 = 0.05 * jax.random.normal(jax.random.fold_in(_tk, 500 + 29), (125000, 16), jnp.float32)
        tbl_30 = 0.05 * jax.random.normal(jax.random.fold_in(_tk, 500 + 30), (125000, 16), jnp.float32)
        tbl_31 = 0.05 * jax.random.normal(jax.random.fold_in(_tk, 500 + 31), (125000, 16), jnp.float32)
        tbl_32 = 0.05 * jax.random.normal(jax.random.fold_in(_tk, 500 + 32), (1000, 16), jnp.float32)
        tbl_33 = 0.05 * jax.random.normal(jax.random.fold_in(_tk, 500 + 33), (1250, 16), jnp.float32)
        tbl_34 = 0.05 * jax.random.normal(jax.random.fold_in(_tk, 500 + 34), (12500, 16), jnp.float32)
        tbl_35 = 0.05 * jax.random.normal(jax.random.fold_in(_tk, 500 + 35), (1000, 16), jnp.float32)
        tbl_36 = 0.05 * jax.random.normal(jax.random.fold_in(_tk, 500 + 36), (1000, 16), jnp.float32)
        tbl_37 = 0.05 * jax.random.normal(jax.random.fold_in(_tk, 500 + 37), (1000, 16), jnp.float32)
        tbl_38 = 0.05 * jax.random.normal(jax.random.fold_in(_tk, 500 + 38), (1000, 16), jnp.float32)
        tbl_39 = 0.05 * jax.random.normal(jax.random.fold_in(_tk, 500 + 39), (1000, 16), jnp.float32)
        _rk = jax.random.fold_in(_tk, 7)
        W_top1 = 0.05 * jax.random.normal(jax.random.fold_in(_tk, 801), (400, 512), jnp.float32)
        W_top2 = 0.0441942 * jax.random.normal(jax.random.fold_in(_tk, 802), (512, 256), jnp.float32)
        W_top3 = 0.0625 * jax.random.normal(jax.random.fold_in(_tk, 803), (256, 1), jnp.float32)
        b_top1 = jnp.zeros((512,), jnp.float32)
        b_top2 = jnp.zeros((256,), jnp.float32)
        return (dense_ctx, ids, tbl_0, tbl_1, tbl_2, tbl_3, tbl_4, tbl_5, tbl_6, tbl_7, tbl_8, tbl_9, tbl_10, tbl_11, tbl_12, tbl_13, tbl_14, tbl_15, tbl_16, tbl_17, tbl_18, tbl_19, tbl_20, tbl_21, tbl_22, tbl_23, tbl_24, tbl_25, tbl_26, tbl_27, tbl_28, tbl_29, tbl_30, tbl_31, tbl_32, tbl_33, tbl_34, tbl_35, tbl_36, tbl_37, tbl_38, tbl_39, W_top1, b_top1, W_top2, b_top2, W_top3)
    dense_ctx, ids, tbl_0, tbl_1, tbl_2, tbl_3, tbl_4, tbl_5, tbl_6, tbl_7, tbl_8, tbl_9, tbl_10, tbl_11, tbl_12, tbl_13, tbl_14, tbl_15, tbl_16, tbl_17, tbl_18, tbl_19, tbl_20, tbl_21, tbl_22, tbl_23, tbl_24, tbl_25, tbl_26, tbl_27, tbl_28, tbl_29, tbl_30, tbl_31, tbl_32, tbl_33, tbl_34, tbl_35, tbl_36, tbl_37, tbl_38, tbl_39, W_top1, b_top1, W_top2, b_top2, W_top3 = _rec_inputs()

    def _L0_rec_setup():
        import jax, jax.numpy as jnp
        import numpy as np
        B, M, D = (512, 40, 16)
        DIMS = [128, 128, 128]
        key = jax.random.key(seed)
        k_x, k0, k1, k2 = jax.random.split(key, 4)
        scale = lambda fan_in: (2.0 / fan_in) ** 0.5
        x0 = jax.random.normal(k_x, (B, M, D), dtype=jnp.float32)
        kern0 = jax.random.normal(k0, (DIMS[0], M, M), dtype=jnp.float32) * scale(M * M)
        kern1 = jax.random.normal(k1, (DIMS[1], DIMS[0], M), dtype=jnp.float32) * scale(DIMS[0] * M)
        kern2 = jax.random.normal(k2, (DIMS[2], DIMS[1], M), dtype=jnp.float32) * scale(DIMS[1] * M)
        return {'x0': x0, 'k0': kern0, 'k1': kern1, 'k2': kern2}
    _L0_rec_all = _L0_rec_setup()
    _L0_rec_in = {k: v for k, v in _L0_rec_all.items() if k in ('k0', 'k1', 'k2')}
    del _L0_rec_all
    return {'dense_ctx': dense_ctx, 'ids': ids, 'tbl_0': tbl_0, 'tbl_1': tbl_1, 'tbl_2': tbl_2, 'tbl_3': tbl_3, 'tbl_4': tbl_4, 'tbl_5': tbl_5, 'tbl_6': tbl_6, 'tbl_7': tbl_7, 'tbl_8': tbl_8, 'tbl_9': tbl_9, 'tbl_10': tbl_10, 'tbl_11': tbl_11, 'tbl_12': tbl_12, 'tbl_13': tbl_13, 'tbl_14': tbl_14, 'tbl_15': tbl_15, 'tbl_16': tbl_16, 'tbl_17': tbl_17, 'tbl_18': tbl_18, 'tbl_19': tbl_19, 'tbl_20': tbl_20, 'tbl_21': tbl_21, 'tbl_22': tbl_22, 'tbl_23': tbl_23, 'tbl_24': tbl_24, 'tbl_25': tbl_25, 'tbl_26': tbl_26, 'tbl_27': tbl_27, 'tbl_28': tbl_28, 'tbl_29': tbl_29, 'tbl_30': tbl_30, 'tbl_31': tbl_31, 'tbl_32': tbl_32, 'tbl_33': tbl_33, 'tbl_34': tbl_34, 'tbl_35': tbl_35, 'tbl_36': tbl_36, 'tbl_37': tbl_37, 'tbl_38': tbl_38, 'tbl_39': tbl_39, 'W_top1': W_top1, 'b_top1': b_top1, 'W_top2': W_top2, 'b_top2': b_top2, 'W_top3': W_top3, 'L0_rec_k0': _L0_rec_in['k0'], 'L0_rec_k1': _L0_rec_in['k1'], 'L0_rec_k2': _L0_rec_in['k2']}

def reference(dense_ctx, ids, tbl_0, tbl_1, tbl_2, tbl_3, tbl_4, tbl_5, tbl_6, tbl_7, tbl_8, tbl_9, tbl_10, tbl_11, tbl_12, tbl_13, tbl_14, tbl_15, tbl_16, tbl_17, tbl_18, tbl_19, tbl_20, tbl_21, tbl_22, tbl_23, tbl_24, tbl_25, tbl_26, tbl_27, tbl_28, tbl_29, tbl_30, tbl_31, tbl_32, tbl_33, tbl_34, tbl_35, tbl_36, tbl_37, tbl_38, tbl_39, W_top1, b_top1, W_top2, b_top2, W_top3, L0_rec_k0, L0_rec_k1, L0_rec_k2):
    import jax
    import jax.numpy as jnp

    def _L0_rec_ref(x0, k0, k1, k2):
        import jax, jax.numpy as jnp
        import numpy as np
        B, M, D = (512, 40, 16)
        DIMS = [128, 128, 128]
        x = x0
        outputs = []
        for k in (k0, k1, k2):
            x = jnp.einsum('bhd,bmd,ohm->bod', x, x0, k)
            outputs.append(jnp.sum(x, axis=-1))
        return jnp.concatenate(outputs, axis=1)
    e = jnp.stack([tbl_0[ids[:, 0]], tbl_1[ids[:, 1]], tbl_2[ids[:, 2]], tbl_3[ids[:, 3]], tbl_4[ids[:, 4]], tbl_5[ids[:, 5]], tbl_6[ids[:, 6]], tbl_7[ids[:, 7]], tbl_8[ids[:, 8]], tbl_9[ids[:, 9]], tbl_10[ids[:, 10]], tbl_11[ids[:, 11]], tbl_12[ids[:, 12]], tbl_13[ids[:, 13]], tbl_14[ids[:, 14]], tbl_15[ids[:, 15]], tbl_16[ids[:, 16]], tbl_17[ids[:, 17]], tbl_18[ids[:, 18]], tbl_19[ids[:, 19]], tbl_20[ids[:, 20]], tbl_21[ids[:, 21]], tbl_22[ids[:, 22]], tbl_23[ids[:, 23]], tbl_24[ids[:, 24]], tbl_25[ids[:, 25]], tbl_26[ids[:, 26]], tbl_27[ids[:, 27]], tbl_28[ids[:, 28]], tbl_29[ids[:, 29]], tbl_30[ids[:, 30]], tbl_31[ids[:, 31]], tbl_32[ids[:, 32]], tbl_33[ids[:, 33]], tbl_34[ids[:, 34]], tbl_35[ids[:, 35]], tbl_36[ids[:, 36]], tbl_37[ids[:, 37]], tbl_38[ids[:, 38]], tbl_39[ids[:, 39]]], axis=1)
    z = _L0_rec_ref(e, L0_rec_k0, L0_rec_k1, L0_rec_k2)
    z = z.reshape(z.shape[0], -1)
    h = jnp.concatenate([z, dense_ctx], axis=1)
    h = jnp.maximum(h @ W_top1 + b_top1, 0.0)
    h = jnp.maximum(h @ W_top2 + b_top2, 0.0)
    y = h @ W_top3
    return y

_drawn_inputs = setup_inputs


def setup_inputs(seed=0):
    import zlib

    import numpy as np

    out = dict(_drawn_inputs(seed))
    spreads = {'b_top1': (0.0, 0.454), 'b_top2': (0.0, 0.1)}
    factors = {'tbl_0': 7.32,
     'tbl_1': 6.952,
     'tbl_2': 6.453,
     'tbl_3': 7.154,
     'tbl_4': 6.554,
     'tbl_5': 6.687,
     'tbl_6': 6.784,
     'tbl_7': 6.979,
     'tbl_8': 6.786,
     'tbl_9': 6.465,
     'tbl_10': 6.939,
     'tbl_11': 6.55,
     'tbl_12': 6.831,
     'tbl_13': 6.825,
     'tbl_14': 6.895,
     'tbl_15': 6.872,
     'tbl_16': 6.639,
     'tbl_17': 5.995,
     'tbl_18': 7.239,
     'tbl_19': 6.612,
     'tbl_20': 7.204,
     'tbl_21': 7.213,
     'tbl_22': 6.854,
     'tbl_23': 6.22,
     'tbl_24': 7.245,
     'tbl_25': 6.652,
     'tbl_26': 6.545,
     'tbl_27': 6.659,
     'tbl_28': 6.414,
     'tbl_29': 7.093,
     'tbl_30': 6.593,
     'tbl_31': 6.799,
     'tbl_32': 6.595,
     'tbl_33': 6.541,
     'tbl_34': 6.963,
     'tbl_35': 6.042,
     'tbl_36': 6.556,
     'tbl_37': 6.444,
     'tbl_38': 7.088,
     'tbl_39': 6.335,
     'L0_rec_k1': 8.0,
     'L0_rec_k2': 8.0}
    for name, (base, spread) in spreads.items():
        noise = np.random.default_rng([zlib.crc32(name.encode()), seed]).standard_normal(out[name].shape)
        drawn = base * np.exp(spread * noise) if base else spread * noise
        out[name] = jnp.asarray(drawn.astype(out[name].dtype))
    for name, factor in factors.items():
        out[name] = (out[name] * factor).astype(out[name].dtype)
    return out
```

```python
from contextlib import ExitStack

import concourse.bass as bass
from concourse import mybir

F32 = mybir.dt.float32
F32R = mybir.dt.float32r
I32 = mybir.dt.int32
ALU = mybir.AluOpType
ACT = mybir.ActivationFunctionType
AX = mybir.AxisListType

P = 128
M, D = 40, 16
LO = 64
KE = LO + M
QC = 512
QB = QC // D
BB = P // D
QUADS = P // QB
JB = QC // P
BLOCKS = P // BB
MC = QC // P
CHUNKS = M // MC
M1 = M + 1

SHIFTS = [(1, 2, 0), (3, 4, M // 2)] + [(s, s + 1, s + 2) for s in range(5, M // 2, 3)]
GROUPS = len(SHIFTS)
GP = 3 * M
REPS = GROUPS + 1

ACT_CHUNKS = (1, 4, 6, 9)
DVE_CHUNKS = tuple(u for u in range(CHUNKS) if u not in ACT_CHUNKS)
NA, ND = len(ACT_CHUNKS), len(DVE_CHUNKS)
NSTT = ND * MC
NSUM = NA + 2
LAG = 2
G_AT = 4

FIRST_AT, SCALARS_AT = 1, 18
REP_AT = {5 + 4 * g: g for g in range(GROUPS)}
L1_AT = {8 + 4 * g: g for g in range(GROUPS)}
TURN_AT = {30 + i: i for i in range(4)}
GATHERS = 3


def cin_tower(nc, dense_t, ids, tables, w1, b1, w2, b2, w3, k0_first, k0_second, k1_t, k2_t, out):
    B = ids.shape[0]
    TILES = B // P
    H1, H2 = w1.shape[1], w2.shape[1]
    F1, F2 = H1 // P, H2 // P
    DC = dense_t.shape[0]

    with ExitStack() as ctx:
        def sb(name, shape, dt=F32):
            return ctx.enter_context(nc.sbuf_tensor(name, shape, dt))

        def sem(name):
            return ctx.enter_context(nc.semaphore(name))

        ids_all = sb("ids_all", [P, TILES, M], I32)
        ids_now = sb("ids_now", [P, M], I32)
        e = sb("e", [P, M * D])
        eT = sb("eT", [KE, P * D], F32R)
        shifted = sb("shifted", [KE, 2 * M])
        sel = sb("sel", [KE, REPS, GP], F32R)
        unit = sb("unit", [KE, M], F32R)
        first = sb("first", [GP, QC])
        pairs = sb("pairs", [GP, GROUPS, QC])
        k0s = sb("k0s", [GP, GROUPS, P])
        k0b = sb("k0b", [GP, GROUPS, P])
        x1h = [sb(f"x1h{i}", [P, QC], F32R) for i in range(2)]
        x1l = [sb(f"x1l{i}", [P, QC], F32R) for i in range(2)]
        ec = [sb(f"ec{i}", [P, JB, M1]) for i in range(2)]
        k1h = sb("k1h", [P, M * P], F32R)
        k1l = sb("k1l", [P, M * P], F32R)
        k2 = sb("k2", [P, M * P])
        scaled = sb("scaled", [P, 2, NA, QC])
        acc = sb("acc", [P, 2, 2, P])
        sums = sb("sums", [P, QC])
        folded = sb("folded", [P, 2 * P])
        x2 = [sb(f"x2{i}", [P, P]) for i in range(2)]
        mask = sb("mask", [P, BB])
        ebd = sb("ebd", [P, BB, M1])
        G = sb("G", [P, M1, P])
        k1_raw = G[:, 0:M, :].rearrange("p m o -> p (m o)")
        ident = sb("ident", [P, P])
        z = [sb(f"z{i}", [P, B]) for i in range(3)]
        dense = sb("dense", [DC, B])
        w1z = sb("w1z", [P, 3, H1])
        w1d = sb("w1d", [DC, H1])
        w2s = sb("w2s", [P, F1, H2])
        w3s = sb("w3s", [P, F2])
        b1s = sb("b1s", [P, F1])
        b2s = sb("b2s", [P, F2])
        h1 = sb("h1", [P, F1, QC])
        h2 = sb("h2", [P, F2, QC])
        y = sb("y", [1, B])

        def bank(name):
            return ctx.enter_context(nc.psum_tensor(name, [P, QC], F32))

        y_act = [bank(f"y_act{i}") for i in range(2)]
        y_dve = [bank(f"y_dve{i}") for i in range(2)]
        rep_ps, x1_ps, g_ps, misc_ps = bank("rep_ps"), bank("x1_ps"), bank("g_ps"), bank("misc_ps")

        ids_in, k0_in, k1_in, late_in = sem("ids_in"), sem("k0_in"), sem("k1_in"), sem("late_in")
        gathered, out_done = sem("gathered"), sem("out_done")
        pool_const, const_ready, k0_ready, k1_ready = sem("pool_const"), sem("const_ready"), sem("k0_ready"), sem("k1_ready")
        ids_ready, ids_seen, turn_seen = sem("ids_ready"), sem("ids_seen"), sem("turn_seen")
        turned, first_rep, scalars_rep, rep_ready, x1_done = (
            sem("turned"), sem("first_rep"), sem("scalars_rep"), sem("rep_ready"), sem("x1_done"))
        ya_ready, yd_ready, g_done, z3_done, mlp_done = (
            sem("ya_ready"), sem("yd_ready"), sem("g_done"), sem("z3_done"), sem("mlp_done"))
        eh_ready, first_ready, ec_ready, x1h_ready = sem("eh_ready"), sem("first_ready"), sem("ec_ready"), sem("x1h_ready")
        scaled_ready, g_out, z3_out, mlp_out = sem("scaled_ready"), sem("g_out"), sem("z3_out"), sem("mlp_out")
        el_ready, pair_ready, x1l_ready, z1_out = sem("el_ready"), sem("pair_ready"), sem("x1l_ready"), sem("z1_out")
        acc_step, yd_used, ebd_ready = sem("acc_step"), sem("yd_used"), sem("ebd_ready")
        sum_step, x2_ready = sem("sum_step"), sem("x2_ready")

        SLOTS = 2

        def scaled_count(n):
            return n + 1 + SLOTS

        def yd_used_count(n):
            return n + 1 + SLOTS

        def x2_count(n):
            return n + 1 + SLOTS

        def g_count(n):
            return n + 1 + SLOTS

        ONE = 1

        block = ctx.enter_context(nc.Block())

        @block.sync
        def _(sp):
            sp.dma_start(ids_all[:], ids.rearrange("(t p) m -> p t m", p=P)).then_inc(ids_in, 16)
            sp.dma_start(k0s[:], k0_first).then_inc(k0_in, 16)
            sp.dma_start(k0b[:], k0_second).then_inc(k0_in, 16)
            sp.dma_start(k1_raw, k1_t).then_inc(k1_in, 16)
            sp.dma_start(k2[:], k2_t).then_inc(late_in, 16)
            sp.dma_start(w1z[:], w1[0:3 * P, :].rearrange("(k p) n -> p k n", p=P)).then_inc(late_in, 16)
            sp.dma_start(w1d[:], w1[3 * P:3 * P + DC, :]).then_inc(late_in, 16)
            sp.dma_start(w2s[:], w2.rearrange("(k p) n -> p k n", p=P)).then_inc(late_in, 16)
            sp.dma_start(w3s[:], w3).then_inc(late_in, 16)
            sp.dma_start(b1s[:], b1).then_inc(late_in, 16)
            sp.dma_start(b2s[:], b2).then_inc(late_in, 16)
            sp.dma_start(dense[:], dense_t).then_inc(late_in, 16)
            LAST = 2 * (F1 + F2 + 1)
            sp.wait_ge(mlp_out, LAST)
            sp.dma_start(out, y[:]).then_inc(out_done, 16)
            sp.wait_ge(out_done, 16)
        LATE = 8 * 16

        @block.gpsimd
        def _(pool):
            def take_ids(t):
                if not (isinstance(t, int) and t == 0):
                    pool.wait_ge(gathered, 16 * M * t)
                nc.gpsimd.tensor_copy(ids_now[:], ids_all[:, t, :] if isinstance(t, int) else
                                      ids_all[:, bass.ds(t, 1), :].rearrange("p a m -> p (a m)")).then_inc(ids_ready, 1)
                pool.wait_ge(ids_ready, t + 1)
                pool.sem_inc(ids_seen, 1)

            def gather(m):
                pool.indirect_dma_start(e[:, m * D:(m + 1) * D], None, tables[m],
                                        bass.IndirectOffsetOnAxis(ap=ids_now[:, m:m + 1], axis=0)).then_inc(gathered, 16)

            pool.sem_inc(x2_ready, SLOTS)
            pool.wait_ge(ids_in, 16)
            take_ids(0)
            for m in range(M):
                gather(m)
            nc.gpsimd.memset(shifted[:], 0.0).then_inc(pool_const, 1)
            nc.gpsimd.memset(mask[:], 1.0).then_inc(pool_const, 1)
            nc.gpsimd.memset(ident[:], 0.0).then_inc(pool_const, 1)
            pool.wait_ge(pool_const, 3)
            view = shifted[:].rearrange("p (a m) -> p a m", a=2)
            nc.gpsimd.affine_select(out=view, in_=view, compare_op=ALU.not_equal, fill=1.0, base=0,
                                    pattern=[[0, 2], [-1, M]], channel_multiplier=1).then_inc(pool_const, 1)
            pool.wait_ge(pool_const, 4)
            nc.gpsimd.affine_select(out=view, in_=view, compare_op=ALU.not_equal, fill=1.0, base=-LO,
                                    pattern=[[0, 2], [-1, M]], channel_multiplier=1).then_inc(pool_const, 1)
            nc.gpsimd.affine_select(out=ident[:], in_=ident[:], compare_op=ALU.not_equal, fill=1.0, base=0,
                                    pattern=[[-1, P]], channel_multiplier=1).then_inc(pool_const, 1)
            nc.gpsimd.affine_select(out=mask[:], in_=mask[:], compare_op=ALU.is_ge, fill=0.0, base=0,
                                    pattern=[[-D, BB]], channel_multiplier=1).then_inc(pool_const, 1)
            pool.wait_ge(pool_const, 7)
            nc.gpsimd.affine_select(out=mask[:], in_=mask[:], compare_op=ALU.is_ge, fill=0.0, base=D - 1,
                                    pattern=[[D, BB]], channel_multiplier=-1).then_inc(pool_const, 1)

            def sum_block(t, k):
                n = t * BLOCKS + k
                s = k % 2
                src = [scaled[:, s, a, :] for a in range(NA)]

                def step(i, dst, a, b):
                    nc.gpsimd.tensor_tensor(dst, a, b, ALU.add).then_inc(sum_step, 1)
                    pool.wait_ge(sum_step, n * (NSUM - 1) + i + 1)

                pool.wait_ge(scaled_ready, scaled_count(n * NA + 1))
                step(0, sums[:], src[0], src[1])
                for a in range(2, NA):
                    pool.wait_ge(scaled_ready, scaled_count(n * NA + a))
                    step(a - 1, sums[:], sums[:], src[a])
                step(NA - 1, folded[:], sums[:, 0:2 * P], sums[:, 2 * P:4 * P])
                pool.wait_ge(acc_step, (n + 1) * NSTT)
                step(NA, folded[:], folded[:], acc[:, s, :, :].rearrange("p a o -> p (a o)"))
                pool.wait_ge(g_done, g_count(n - SLOTS))
                nc.gpsimd.tensor_tensor(x2[s][:], folded[:, 0:P], folded[:, P:2 * P], ALU.add).then_inc(x2_ready, 1)

            def tile_body(t, last):
                if not last:
                    pool.wait_ge(turned, QUADS * (t + 1))
                    take_ids(t + 1)
                m = 0
                for k in range(BLOCKS):
                    if not last:
                        while m < min(M, GATHERS * (k + 1) + (k == M // GATHERS - 1)):
                            gather(m)
                            m += 1
                    sum_block(t, k)

            with pool.Fori(0, TILES - 1) as t:
                tile_body(t, False)
            tile_body(TILES - 1, True)

        @block.tensor
        def _(pe):
            def transpose_part(t, i):
                if i == 0:
                    pe.wait_ge(gathered, 16 * M * (t + 1))
                    pe.wait_ge(ec_ready, QUADS * t)
                else:
                    pe.wait_ge(el_ready, QUADS * t + i)
                pe.sem_inc(turn_seen, 1)
                for dd in range(4):
                    ins = nc.tensor.transpose(misc_ps[0:M, dd * P:(dd + 1) * P],
                                              e[:].rearrange("p (m d) -> p d m", d=D)[:, 4 * i + dd, :], ident[:])
                ins.then_inc(turned, 1)

            def e_cols(q):
                return eT[:, q * QC:(q + 1) * QC]

            def first_factor(n, q):
                pe.wait_ge(el_ready, n - q + QUADS)
                pe.wait_ge(pair_ready, GROUPS * n)
                nc.tensor.matmul(rep_ps[0:GP, :], sel[:, GROUPS, :], e_cols(q), start=True, stop=True).then_inc(first_rep, 1)

            def scalars(n, q):
                if q == 0:
                    pe.wait_ge(el_ready, n + QUADS)
                elif q == 1:
                    pe.wait_ge(z3_out, ONE + n_tile[0])
                else:
                    pe.wait_ge(ec_ready, n)
                for j in range(JB):
                    ins = nc.tensor.matmul(misc_ps[:, j * M:(j + 1) * M], eT[:, q * QC + j * P:q * QC + (j + 1) * P],
                                           unit[:], start=True, stop=True)
                ins.then_inc(scalars_rep, 1)

            n_tile = [0]

            def rep(n, q, g):
                if g == 0:
                    pe.wait_ge(first_ready, n + 1)
                else:
                    pe.wait_ge(pair_ready, GROUPS * n + g)
                nc.tensor.matmul(rep_ps[0:GP, :], sel[:, g, :], e_cols(q), start=True, stop=True).then_inc(rep_ready, 1)

            def layer1(n, g):
                pe.wait_ge(pair_ready, GROUPS * n + g + 1)
                if g == 0:
                    pe.wait_ge(z1_out, n)
                ins = nc.tensor.matmul(x1_ps[:], k0s[:, g, :], pairs[:, g, :], start=(g == 0), stop=(g == GROUPS - 1))
                if g == GROUPS - 1:
                    ins.then_inc(x1_done, 1)

            def layer2(t, k, u):
                n = t * BLOCKS + k
                s, j = (k // JB) % 2, k % JB
                if j == 0 and u == 0:
                    quad = t * QUADS + k // JB
                    pe.wait_ge(x1h_ready, quad + 1)
                    pe.wait_ge(x1l_ready, quad + 1)
                hi, lo = x1h[s][:, j * P:(j + 1) * P], x1l[s][:, j * P:(j + 1) * P]
                cols = slice(u * QC, (u + 1) * QC)
                if u in ACT_CHUNKS:
                    i = n * NA + ACT_CHUNKS.index(u)
                    pe.wait_ge(scaled_ready, scaled_count(i - 2))
                    dst, ready = y_act[(ACT_CHUNKS.index(u) + k * NA) % 2], ya_ready
                else:
                    i = n * ND + DVE_CHUNKS.index(u)
                    pe.wait_ge(yd_used, yd_used_count(i - 2))
                    dst, ready = y_dve[(DVE_CHUNKS.index(u) + k * ND) % 2], yd_ready
                nc.tensor.matmul(dst[:], hi, k1h[:, cols], start=True, stop=False)
                nc.tensor.matmul(dst[:], hi, k1l[:, cols], start=False, stop=False)
                nc.tensor.matmul(dst[:], lo, k1h[:, cols], start=False, stop=True).then_inc(ready, 1)

            def gram(t, k):
                n = t * BLOCKS + k
                pe.wait_ge(x2_ready, x2_count(n))
                pe.wait_ge(ebd_ready, ONE + n + 1)
                pe.wait_ge(g_out, ONE + n)
                nc.tensor.matmul(g_ps[:, 0:BB * M1], x2[k % 2][:], ebd[:].rearrange("p b m -> p (b m)"),
                                 start=True, stop=True).then_inc(g_done, 1)

            def layer3(t):
                pe.wait_ge(g_out, ONE + (t + 1) * BLOCKS)
                for m in range(M):
                    ins = nc.tensor.matmul(misc_ps[:, 0:P], k2[:, m * P:(m + 1) * P], G[:, m, :],
                                           start=(m == 0), stop=(m == M - 1))
                ins.then_inc(z3_done, 1)

            def tile_body(t, last):
                n_tile[0] = t
                for k in range(BLOCKS):
                    q = k // JB
                    for u in range(CHUNKS):
                        layer2(t, k, u)
                        if u == G_AT and k >= LAG:
                            gram(t, k - LAG)
                        at = (k % JB) * CHUNKS + u
                        if q < QUADS - 1:
                            n = t * QUADS + q + 1
                            if at == FIRST_AT:
                                first_factor(n, q + 1)
                            elif at == SCALARS_AT:
                                scalars(n, q + 1)
                            elif at in REP_AT:
                                rep(n, q + 1, REP_AT[at])
                            elif at in L1_AT:
                                layer1(n, L1_AT[at])
                        elif not last and at in TURN_AT:
                            transpose_part(t + 1, TURN_AT[at])
                if not last:
                    n = (t + 1) * QUADS
                    first_factor(n, 0)
                    scalars(n, 0)
                    for g in range(GROUPS):
                        rep(n, 0, g)
                        if g == 1:
                            gram(t, BLOCKS - 2)
                        if g >= 1:
                            layer1(n, g - 1)
                    gram(t, BLOCKS - 1)
                    layer1(n, GROUPS - 1)
                    pe.wait_ge(ec_ready, n + 1)
                else:
                    gram(t, BLOCKS - 2)
                    gram(t, BLOCKS - 1)
                layer3(t)

            pe.sem_inc(g_done, SLOTS)
            pe.sem_inc(z3_done, ONE)
            pe.sem_inc(ya_ready, ONE)
            pe.wait_ge(const_ready, 1)
            pe.wait_ge(pool_const, 8)
            for i in range(4):
                transpose_part(0, i)
            first_factor(0, 0)
            scalars(0, 0)
            pe.wait_ge(k0_ready, 1)
            for g in range(GROUPS):
                rep(0, 0, g)
                if g >= 1:
                    layer1(0, g - 1)
            layer1(0, GROUPS - 1)
            pe.wait_ge(k1_ready, 1)
            pe.wait_ge(late_in, LATE)
            with pe.Fori(0, TILES - 1) as t:
                tile_body(t, False)
            tile_body(TILES - 1, True)

            pe.wait_ge(z3_out, ONE + TILES)
            pe.wait_ge(z1_out, TILES * QUADS)
            done = 0
            banks = [y_act[0], y_act[1], y_dve[0], y_dve[1], rep_ps, x1_ps, g_ps]
            for half in range(2):
                cols = slice(half * QC, (half + 1) * QC)
                for f in range(F1):
                    if half:
                        pe.wait_ge(mlp_out, done - len(banks) + 1)
                    ps = banks[done % 7]
                    fs = slice(f * P, (f + 1) * P)
                    for i in range(3):
                        nc.tensor.matmul(ps[:], w1z[:, i, fs], z[i][:, cols], start=(i == 0), stop=False)
                    nc.tensor.matmul(ps[:], w1d[:, fs], dense[:, cols], start=False, stop=True).then_inc(mlp_done, 1)
                    done += 1
                for f in range(F2):
                    ps = banks[done % 7]
                    for i in range(F1):
                        if f == 0:
                            pe.wait_ge(mlp_out, half * (F1 + F2 + 1) + i + 1)
                        ins = nc.tensor.matmul(ps[:], w2s[:, i, f * P:(f + 1) * P], h1[:, i, :],
                                               start=(i == 0), stop=(i == F1 - 1))
                    ins.then_inc(mlp_done, 1)
                    done += 1
                ps = banks[done % 7]
                for i in range(F2):
                    pe.wait_ge(mlp_out, half * (F1 + F2 + 1) + F1 + i + 1)
                    ins = nc.tensor.matmul(ps[0:1, :], w3s[:, i:i + 1], h2[:, i, :], start=(i == 0), stop=(i == F2 - 1))
                ins.then_inc(mlp_done, 1)
                done += 1

        @block.scalar
        def _(act):
            def high_part(t, i):
                act.wait_ge(turned, QUADS * t + i + 1)
                if i == 0:
                    act.wait_ge(x1_done, QUADS * t)
                nc.scalar.copy(eT[0:M, :].rearrange("p (b d) -> p d b", d=D)[:, 4 * i:4 * i + 4, :],
                               misc_ps[0:M, :].rearrange("p (d b) -> p d b", d=4)).then_inc(eh_ready, 1)

            def take_first(n):
                act.wait_ge(first_rep, n + 1)
                act.wait_ge(pair_ready, GROUPS * n)
                nc.scalar.copy(first[:], rep_ps[0:GP, :]).then_inc(first_ready, 1)

            def take_scalars(n, q):
                act.wait_ge(scalars_rep, n + 1)
                if not (isinstance(n, int) and n == 0):
                    act.wait_ge(ebd_ready, ONE + JB * (n - 1))
                nc.scalar.copy(ec[q % 2][:, :, 0:M], misc_ps[:, 0:JB * M].rearrange("p (j m) -> p j m", j=JB))\
                    .then_inc(ec_ready, 1)

            def take_x1(n, q):
                act.wait_ge(x1_done, n + 1)
                if not (isinstance(n, int) and n == 0):
                    act.wait_ge(ya_ready, ONE + NA * JB * (n - 1))
                nc.scalar.copy(x1h[q % 2][:], x1_ps[:]).then_inc(x1h_ready, 1)

            def scale_chunk(t, k, u):
                n = t * BLOCKS + k
                a = ACT_CHUNKS.index(u)
                q, j = k // JB, k % JB
                act.wait_ge(ya_ready, ONE + n * NA + a + 1)
                if j == 0 and a == 0:
                    act.wait_ge(ec_ready, t * QUADS + q + 1)
                if a == 0:
                    act.wait_ge(x2_ready, x2_count(n - SLOTS))
                ps = y_act[(a + k * NA) % 2]
                for i in range(MC):
                    m = u * MC + i
                    ins = nc.scalar.activation(scaled[:, k % 2, a, i * P:(i + 1) * P], ps[:, i * P:(i + 1) * P], ACT.Copy,
                                               scale=ec[q % 2][:, j, m:m + 1])
                ins.then_inc(scaled_ready, 1)

            def take_gram(t, k):
                n = t * BLOCKS + k
                act.wait_ge(g_done, g_count(n))
                if k == 0:
                    act.wait_ge(z3_done, ONE + t)
                nc.scalar.copy(G[:, :, k * BB:(k + 1) * BB],
                               g_ps[:, 0:BB * M1].rearrange("p (b m) -> p m b", m=M1)).then_inc(g_out, 1)

            def samples(t):
                return slice(t * P, (t + 1) * P) if isinstance(t, int) else bass.ds(t * P, P)

            def tile_body(t, last):
                for k in range(BLOCKS):
                    q = k // JB
                    for u in range(CHUNKS):
                        if u in ACT_CHUNKS:
                            scale_chunk(t, k, u)
                        if u == G_AT + 1 and k >= LAG:
                            take_gram(t, k - LAG)
                        at = (k % JB) * CHUNKS + u
                        if q < QUADS - 1:
                            n = t * QUADS + q + 1
                            if at == FIRST_AT:
                                take_first(n)
                            elif at == SCALARS_AT:
                                take_scalars(n, q + 1)
                            elif L1_AT.get(at) == GROUPS - 1:
                                take_x1(n, q + 1)
                        elif not last and at in TURN_AT:
                            high_part(t + 1, TURN_AT[at])
                if not last:
                    n = (t + 1) * QUADS
                    take_first(n)
                    take_scalars(n, 0)
                    take_gram(t, BLOCKS - 2)
                    take_gram(t, BLOCKS - 1)
                    take_x1(n, 0)
                else:
                    take_gram(t, BLOCKS - 2)
                    take_gram(t, BLOCKS - 1)
                act.wait_ge(g_out, ONE + (t + 1) * BLOCKS)
                nc.scalar.copy(z[1][:, samples(t)], G[:, M, :])
                act.wait_ge(z3_done, ONE + t + 1)
                nc.scalar.copy(z[2][:, samples(t)], misc_ps[:, 0:P]).then_inc(z3_out, 1)

            act.sem_inc(scaled_ready, SLOTS)
            act.sem_inc(g_out, ONE)
            act.sem_inc(z3_out, ONE)
            act.wait_ge(const_ready, 1)
            for i in range(4):
                high_part(0, i)
            take_first(0)
            take_scalars(0, 0)
            take_x1(0, 0)
            with act.Fori(0, TILES - 1) as t:
                tile_body(t, False)
            tile_body(TILES - 1, True)

            act.wait_ge(late_in, LATE)
            done = 0
            banks = [y_act[0], y_act[1], y_dve[0], y_dve[1], rep_ps, x1_ps, g_ps]
            for half in range(2):
                for f in range(F1):
                    act.wait_ge(mlp_done, done + 1)
                    if half and f == 0:
                        act.wait_ge(mlp_done, F1 + F2 + 1)
                    nc.scalar.activation(h1[:, f, :], banks[done % 7][:], ACT.Relu, bias=b1s[:, f:f + 1]).then_inc(mlp_out, 1)
                    done += 1
                for f in range(F2):
                    act.wait_ge(mlp_done, done + 1)
                    nc.scalar.activation(h2[:, f, :], banks[done % 7][:], ACT.Relu, bias=b2s[:, f:f + 1]).then_inc(mlp_out, 1)
                    done += 1
                act.wait_ge(mlp_done, done + 1)
                nc.scalar.copy(y[:, half * QC:(half + 1) * QC], banks[done % 7][0:1, :]).then_inc(mlp_out, 1)
                done += 1

        @block.vector
        def _(dve):
            def low_part(t, i):
                dve.wait_ge(eh_ready, QUADS * t + i + 1)
                hi = eT[0:M, :].rearrange("p (b d) -> p d b", d=D)[:, 4 * i:4 * i + 4, :].bitcast(F32)
                lo = eT[LO:KE, :].rearrange("p (b d) -> p d b", d=D)[:, 4 * i:4 * i + 4, :]
                nc.vector.tensor_tensor(lo, misc_ps[0:M, :].rearrange("p (d b) -> p d b", d=4), hi, ALU.subtract)\
                    .then_inc(el_ready, 1)

            def pair(n, g):
                dve.wait_ge(rep_ready, GROUPS * n + g + 1)
                if g == 0:
                    dve.wait_ge(first_ready, n + 1)
                    dve.wait_ge(x1_done, n)
                nc.vector.tensor_tensor(pairs[:, g, :], rep_ps[0:GP, :], first[:], ALU.mult).then_inc(pair_ready, 1)

            def take_x1(t, n, q):
                dve.wait_ge(x1h_ready, n + 1)
                nc.vector.tensor_tensor(x1l[q % 2][:], x1_ps[:], x1h[q % 2][:].bitcast(F32), ALU.subtract)\
                    .then_inc(x1l_ready, 1)
                cols = slice(q * QB, (q + 1) * QB) if isinstance(n, int) else bass.ds(t * P + q * QB, QB)
                if isinstance(n, int):
                    cols = slice(n * QB, (n + 1) * QB)
                nc.vector.tensor_reduce(z[0][:, cols], x1_ps[:].rearrange("p (b d) -> p b d", d=D), AX.X, ALU.add)\
                    .then_inc(z1_out, 1)

            def sum_chunk(t, k, u):
                n = t * BLOCKS + k
                c = DVE_CHUNKS.index(u)
                q, j = k // JB, k % JB
                dve.wait_ge(yd_ready, n * ND + c + 1)
                if j == 0 and c == 0:
                    dve.wait_ge(ec_ready, t * QUADS + q + 1)
                if c == 0:
                    dve.wait_ge(x2_ready, x2_count(n - SLOTS))
                ps = y_dve[(c + k * ND) % 2]
                for i in range(MC):
                    m, step = u * MC + i, c * MC + i
                    into = acc[:, k % 2, step % 2, :]
                    scalar = ec[q % 2][:, j, m:m + 1]
                    if step < 2:
                        ins = nc.vector.tensor_scalar(into, ps[:, i * P:(i + 1) * P], scalar, None, ALU.mult)
                    else:
                        dve.wait_ge(acc_step, n * NSTT + step - 1)
                        ins = nc.vector.scalar_tensor_tensor(out=into, in0=ps[:, i * P:(i + 1) * P], scalar=scalar,
                                                             in1=into, op0=ALU.mult, op1=ALU.add)
                    ins.then_inc(acc_step, 1)
                    if i == MC - 1:
                        dve.wait_ge(acc_step, n * NSTT + step + 1)
                        dve.sem_inc(yd_used, 1)

            def diagonal(t, k):
                n = t * BLOCKS + k
                q, j = k // JB, k % JB
                dve.wait_ge(g_done, g_count(n - 1))
                nc.vector.tensor_tensor(ebd[:], ec[q % 2][:, j:j + 1, :].to_broadcast([P, BB, M1]),
                                        mask[:].rearrange("p (b a) -> p b a", a=1).to_broadcast([P, BB, M1]), ALU.mult)\
                    .then_inc(ebd_ready, 1)

            def tile_body(t, last):
                for k in range(BLOCKS):
                    q = k // JB
                    for u in range(CHUNKS):
                        if u in DVE_CHUNKS:
                            sum_chunk(t, k, u)
                        if u == G_AT - 1 and k >= LAG:
                            diagonal(t, k - LAG)
                        at = (k % JB) * CHUNKS + u
                        if q < QUADS - 1:
                            n = t * QUADS + q + 1
                            if at in REP_AT:
                                pair(n, REP_AT[at])
                            elif L1_AT.get(at) == GROUPS - 1:
                                take_x1(t, n, q + 1)
                        elif not last and at in TURN_AT:
                            low_part(t + 1, TURN_AT[at])
                if not last:
                    n = (t + 1) * QUADS
                    pair(n, 0)
                    diagonal(t, BLOCKS - 2)
                    for g in range(1, GROUPS):
                        pair(n, g)
                    diagonal(t, BLOCKS - 1)
                    take_x1(t + 1, n, 0)
                else:
                    diagonal(t, BLOCKS - 2)
                    diagonal(t, BLOCKS - 1)

            dve.sem_inc(yd_used, SLOTS)
            dve.sem_inc(ebd_ready, ONE)
            nc.vector.memset(eT[32:LO, :].bitcast(F32), 0.0)
            for i in range(2):
                nc.vector.memset(ec[i][:, :, M:M1], 1.0)
            dve.wait_ge(k1_in, 16)
            nc.vector.tensor_copy(k1h[:], k1_raw).then_inc(k1_ready, 1)
            dve.wait_ge(k1_ready, 1)
            nc.vector.tensor_tensor(k1l[:], k1_raw, k1h[:].bitcast(F32), ALU.subtract)
            dve.wait_ge(k0_in, 32)
            nc.vector.tensor_tensor(k0s[0:2 * M, 0:2, :], k0s[0:2 * M, 0:2, :], k0b[0:2 * M, 0:2, :], ALU.add)
            nc.vector.tensor_tensor(k0s[:, 2:, :], k0s[:, 2:, :], k0b[:, 2:, :], ALU.add).then_inc(k0_ready, 1)
            dve.wait_ge(pool_const, 8)
            for g in range(GROUPS):
                for a in range(3):
                    s = SHIFTS[g][a]
                    nc.vector.tensor_copy(sel[:, g, a * M:(a + 1) * M], shifted[:, s:s + M])
            for a in range(3):
                nc.vector.tensor_copy(sel[:, GROUPS, a * M:(a + 1) * M], shifted[:, 0:M])
            nc.vector.tensor_copy(unit[:], shifted[:, 0:M]).then_inc(const_ready, 1)
            for i in range(4):
                low_part(0, i)
            for g in range(GROUPS):
                pair(0, g)
            take_x1(0, 0, 0)
            with dve.Fori(0, TILES - 1) as t:
                tile_body(t, False)
            tile_body(TILES - 1, True)


def kernel(**inputs):
    import numpy as np
    import concourse.bacc as bacc
    from concourse.bass_utils import run_bass_kernel_spmd

    a = {k: np.asarray(v) for k, v in inputs.items()}
    tables = [a[f"tbl_{m}"] for m in range(M)]
    k0, k1, k2 = a["L0_rec_k0"], a["L0_rec_k1"], a["L0_rec_k2"]
    m = np.arange(M)
    pair = np.array([[(m + s) % M for s in group] for group in SHIFTS])
    own = np.broadcast_to(m, pair.shape)
    k0_first = k0[:, own, pair].transpose(2, 3, 1, 0).reshape(GP, GROUPS, P)
    k0_second = k0[:, pair, own].transpose(2, 3, 1, 0).reshape(GP, GROUPS, P)
    H1, H2 = a["W_top2"].shape
    arrays = {
        "dense_t": a["dense_ctx"].T, "ids": a["ids"],
        **{f"tbl_{i}": v for i, v in enumerate(tables)},
        "w1": a["W_top1"], "b1": a["b_top1"].reshape(H1 // P, P).T, "w2": a["W_top2"],
        "b2": a["b_top2"].reshape(H2 // P, P).T, "w3": a["W_top3"].reshape(H2 // P, P).T,
        "k0_first": k0_first, "k0_second": k0_second,
        "k1_t": k1.transpose(1, 2, 0).reshape(P, M * P), "k2_t": k2.transpose(1, 2, 0).reshape(P, M * P),
    }
    arrays = {k: np.ascontiguousarray(v) for k, v in arrays.items()}
    nc = bacc.Bacc("TRN2", target_bir_lowering=False, num_devices=1)
    ap = {k: nc.dram_tensor("in_" + k, v.shape, mybir.dt.from_np(v.dtype), kind="ExternalInput").ap()
          for k, v in arrays.items()}
    B = a["ids"].shape[0]
    out = nc.dram_tensor("out_y", (1, B), F32, kind="ExternalOutput").ap()
    cin_tower(nc, ap["dense_t"], ap["ids"], [ap[f"tbl_{i}"] for i in range(M)], ap["w1"], ap["b1"], ap["w2"], ap["b2"],
              ap["w3"], ap["k0_first"], ap["k0_second"], ap["k1_t"], ap["k2_t"], out)
    r = run_bass_kernel_spmd(nc, [{"in_" + k: v for k, v in arrays.items()}], core_ids=[0])
    return r.results[0]["out_y"].reshape(B, 1)
```

```python
from contextlib import ExitStack

import concourse.bass as bass
from concourse import mybir

F32 = mybir.dt.float32
F32R = mybir.dt.float32r
I32 = mybir.dt.int32
ALU = mybir.AluOpType
ACT = mybir.ActivationFunctionType
AX = mybir.AxisListType

P = 128
M, D = 40, 16
LO = 64
KE = LO + M
QC = 512
QB = QC // D
BB = P // D
QUADS = P // QB
JB = QC // P
BLOCKS = P // BB
MC = QC // P
CHUNKS = M // MC
M1 = M + 1

SHIFTS = [(1, 2, 0), (3, 4, M // 2)] + [(s, s + 1, s + 2) for s in range(5, M // 2, 3)]
GROUPS = len(SHIFTS)
GP = 3 * M
REPS = GROUPS + 1

SHARES = {4: (1, 4, 6, 9), 5: (1, 3, 5, 7, 9), 6: (0, 2, 4, 6, 8, 9)}
NA = [4] * 16
ACT_CHUNKS = [SHARES[n] for n in NA]
DVE_CHUNKS = [tuple(u for u in range(CHUNKS) if u not in c) for c in ACT_CHUNKS]
ND = [CHUNKS - n for n in NA]
NA_TILE, ND_TILE = sum(NA), sum(ND)
YA, YD = 2, 3
assert len(NA) == BLOCKS and NA_TILE % YA == 0 and ND_TILE % YD == 0
LAG = 2
G_AT = 4
HEAD = LAG + 1

FIRST_AT, SCALARS_AT = 1, 34
REP_AT = {5 + 4 * g: g for g in range(GROUPS)}
L1_AT = {8 + 4 * g: g for g in range(GROUPS)}
TURN_AT = {18 + i: i for i in range(4)}
LAST_SCALARS_AT, LAST_FIRST_AT = 22, 23
LAST_REP_AT = {24 + 2 * g: g for g in range(GROUPS)}
LAST_L1_AT = {26 + 2 * g: g for g in range(GROUPS)}
L3_AT = {16 + i: i for i in range(8)}
GATHERS = 4


def front_steps(k, u):
    at = (k % JB) * CHUNKS + u
    if k // JB < QUADS - 1:
        where = {"first": {FIRST_AT: 0}, "rep": REP_AT, "layer1": L1_AT, "scalars": {SCALARS_AT: 0}}
    else:
        where = {"turn": TURN_AT, "scalars": {LAST_SCALARS_AT: 0}, "first": {LAST_FIRST_AT: 0},
                 "rep": LAST_REP_AT, "layer1": LAST_L1_AT}
    return {name: slots[at] for name, slots in where.items() if at in slots}


def cin_tower(nc, dense_t, ids, tables, w1, b1, w2, b2, w3, k0_first, k0_second, k1_t, k2_t, out):
    B = ids.shape[0]
    TILES = B // P
    H1, H2 = w1.shape[1], w2.shape[1]
    F1, F2 = H1 // P, H2 // P
    DC = dense_t.shape[0]

    with ExitStack() as ctx:
        def sb(name, shape, dt=F32):
            return ctx.enter_context(nc.sbuf_tensor(name, shape, dt))

        def sem(name):
            return ctx.enter_context(nc.semaphore(name))

        ids_all = sb("ids_all", [P, TILES, M], I32)
        ids_now = sb("ids_now", [P, M], I32)
        e = sb("e", [P, M * D])
        eT = sb("eT", [KE, P * D], F32R)
        shifted = sb("shifted", [KE, 2 * M])
        sel = sb("sel", [KE, REPS, GP], F32R)
        unit = sb("unit", [KE, M], F32R)
        first = sb("first", [GP, QC])
        pairs = sb("pairs", [GP, GROUPS, QC])
        k0s = sb("k0s", [GP, GROUPS, P])
        k0b = sb("k0b", [GP, GROUPS, P])
        x1h = [sb(f"x1h{i}", [P, QC], F32R) for i in range(2)]
        x1l = [sb(f"x1l{i}", [P, QC], F32R) for i in range(2)]
        ec = [sb(f"ec{i}", [P, JB, M1]) for i in range(2)]
        k1h = sb("k1h", [P, M * P], F32R)
        k1l = sb("k1l", [P, M * P], F32R)
        k2 = sb("k2", [P, M * P])
        scaled = sb("scaled", [P, 2, max(NA), QC])
        acc = sb("acc", [P, 2, 2, P])
        sums = sb("sums", [P, QC])
        folded = sb("folded", [P, 2 * P])
        x2 = [sb(f"x2{i}", [P, P]) for i in range(2)]
        mask = sb("mask", [P, BB])
        ebd = sb("ebd", [P, BB, M1])
        G = sb("G", [P, M1, P])
        k1_raw = G[:, 0:M, :].rearrange("p m o -> p (m o)")
        ident = sb("ident", [P, P])
        z = [sb(f"z{i}", [P, B]) for i in range(3)]
        dense = sb("dense", [DC, B])
        w1z = sb("w1z", [P, 3, H1])
        w1d = sb("w1d", [DC, H1])
        w2s = sb("w2s", [P, F1, H2])
        w3s = sb("w3s", [P, F2])
        b1s = sb("b1s", [P, F1])
        b2s = sb("b2s", [P, F2])
        h1 = sb("h1", [P, F1, QC])
        h2 = sb("h2", [P, F2, QC])
        y = sb("y", [1, B])

        def bank(name):
            return ctx.enter_context(nc.psum_tensor(name, [P, QC], F32))

        y_act = [bank(f"y_act{i}") for i in range(YA)]
        y_dve = [bank(f"y_dve{i}") for i in range(YD)]
        rep_ps, x1_ps, g_ps = bank("rep_ps"), bank("x1_ps"), bank("g_ps")
        mlp_banks = [*y_act, *y_dve, rep_ps, x1_ps]

        ids_in, k0_in, k1_in, late_in = sem("ids_in"), sem("k0_in"), sem("k1_in"), sem("late_in")
        gathered, out_done = sem("gathered"), sem("out_done")
        pool_const, const_ready, k0_ready, k1_ready = sem("pool_const"), sem("const_ready"), sem("k0_ready"), sem("k1_ready")
        ids_ready, ids_seen, turn_seen = sem("ids_ready"), sem("ids_seen"), sem("turn_seen")
        turned, first_rep, scalars_rep, rep_ready, x1_done = (
            sem("turned"), sem("first_rep"), sem("scalars_rep"), sem("rep_ready"), sem("x1_done"))
        ya_ready, yd_ready, g_done, z3_done, mlp_done = (
            sem("ya_ready"), sem("yd_ready"), sem("g_done"), sem("z3_done"), sem("mlp_done"))
        eh_ready, first_ready, ec_ready, x1h_ready = sem("eh_ready"), sem("first_ready"), sem("ec_ready"), sem("x1h_ready")
        scaled_ready, g_out, z3_out, mlp_out = sem("scaled_ready"), sem("g_out"), sem("z3_out"), sem("mlp_out")
        el_ready, pair_ready, x1l_ready, z1_out = sem("el_ready"), sem("pair_ready"), sem("x1l_ready"), sem("z1_out")
        acc_step, ebd_ready = sem("acc_step"), sem("ebd_ready")
        sum_step, x2_ready = sem("sum_step"), sem("x2_ready")

        SLOTS = 2

        def act_chunk(t, k, a=0):
            return t * NA_TILE + sum(NA[:k]) + a

        def dve_chunk(t, k, c=0):
            return t * ND_TILE + sum(ND[:k]) + c

        def scaled_count(chunk):
            return chunk + 1 + YA

        def acc_count(chunk, step=MC - 1):
            return (chunk + YD) * MC + step + 1

        def x2_count(n):
            return n + 1 + SLOTS

        def g_count(n):
            return n + 1 + SLOTS

        ONE = 1

        block = ctx.enter_context(nc.Block())

        @block.sync
        def _(sp):
            sp.dma_start(ids_all[:], ids.rearrange("(t p) m -> p t m", p=P)).then_inc(ids_in, 16)
            sp.dma_start(k0s[:], k0_first).then_inc(k0_in, 16)
            sp.dma_start(k0b[:], k0_second).then_inc(k0_in, 16)
            sp.dma_start(k1_raw, k1_t).then_inc(k1_in, 16)
            sp.dma_start(k2[:], k2_t).then_inc(late_in, 16)
            sp.dma_start(w1z[:], w1[0:3 * P, :].rearrange("(k p) n -> p k n", p=P)).then_inc(late_in, 16)
            sp.dma_start(w1d[:], w1[3 * P:3 * P + DC, :]).then_inc(late_in, 16)
            sp.dma_start(w2s[:], w2.rearrange("(k p) n -> p k n", p=P)).then_inc(late_in, 16)
            sp.dma_start(w3s[:], w3).then_inc(late_in, 16)
            sp.dma_start(b1s[:], b1).then_inc(late_in, 16)
            sp.dma_start(b2s[:], b2).then_inc(late_in, 16)
            sp.dma_start(dense[:], dense_t).then_inc(late_in, 16)
            LAST = 2 * (F1 + F2 + 1)
            sp.wait_ge(mlp_out, LAST)
            sp.dma_start(out, y[:]).then_inc(out_done, 16)
            sp.wait_ge(out_done, 16)
        LATE = 8 * 16

        @block.gpsimd
        def _(pool):
            def take_ids(t):
                if not (isinstance(t, int) and t == 0):
                    pool.wait_ge(gathered, 16 * M * t)
                nc.gpsimd.tensor_copy(ids_now[:], ids_all[:, t, :] if isinstance(t, int) else
                                      ids_all[:, bass.ds(t, 1), :].rearrange("p a m -> p (a m)")).then_inc(ids_ready, 1)
                pool.wait_ge(ids_ready, t + 1)
                pool.sem_inc(ids_seen, 1)

            def gather(m):
                pool.indirect_dma_start(e[:, m * D:(m + 1) * D], None, tables[m],
                                        bass.IndirectOffsetOnAxis(ap=ids_now[:, m:m + 1], axis=0)).then_inc(gathered, 16)

            pool.sem_inc(x2_ready, SLOTS)
            pool.wait_ge(ids_in, 16)
            take_ids(0)
            for m in range(M):
                gather(m)
            nc.gpsimd.memset(shifted[:], 0.0).then_inc(pool_const, 1)
            nc.gpsimd.memset(mask[:], 1.0).then_inc(pool_const, 1)
            nc.gpsimd.memset(ident[:], 0.0).then_inc(pool_const, 1)
            pool.wait_ge(pool_const, 3)
            view = shifted[:].rearrange("p (a m) -> p a m", a=2)
            nc.gpsimd.affine_select(out=view, in_=view, compare_op=ALU.not_equal, fill=1.0, base=0,
                                    pattern=[[0, 2], [-1, M]], channel_multiplier=1).then_inc(pool_const, 1)
            pool.wait_ge(pool_const, 4)
            nc.gpsimd.affine_select(out=view, in_=view, compare_op=ALU.not_equal, fill=1.0, base=-LO,
                                    pattern=[[0, 2], [-1, M]], channel_multiplier=1).then_inc(pool_const, 1)
            nc.gpsimd.affine_select(out=ident[:], in_=ident[:], compare_op=ALU.not_equal, fill=1.0, base=0,
                                    pattern=[[-1, P]], channel_multiplier=1).then_inc(pool_const, 1)
            nc.gpsimd.affine_select(out=mask[:], in_=mask[:], compare_op=ALU.is_ge, fill=0.0, base=0,
                                    pattern=[[-D, BB]], channel_multiplier=1).then_inc(pool_const, 1)
            pool.wait_ge(pool_const, 7)
            nc.gpsimd.affine_select(out=mask[:], in_=mask[:], compare_op=ALU.is_ge, fill=0.0, base=D - 1,
                                    pattern=[[D, BB]], channel_multiplier=-1).then_inc(pool_const, 1)

            def sum_block(t, k):
                n = t * BLOCKS + k
                s, na = k % 2, NA[k]
                src = [scaled[:, s, a, :] for a in range(na)]
                before = t * (NA_TILE + BLOCKS) + sum(NA[:k]) + k

                def step(i, dst, a, b):
                    nc.gpsimd.tensor_tensor(dst, a, b, ALU.add).then_inc(sum_step, 1)
                    pool.wait_ge(sum_step, before + i + 1)

                pool.wait_ge(scaled_ready, scaled_count(act_chunk(t, k, 1)))
                step(0, sums[:], src[0], src[1])
                for a in range(2, na):
                    pool.wait_ge(scaled_ready, scaled_count(act_chunk(t, k, a)))
                    step(a - 1, sums[:], sums[:], src[a])
                step(na - 1, folded[:], sums[:, 0:2 * P], sums[:, 2 * P:4 * P])
                pool.wait_ge(acc_step, acc_count(dve_chunk(t, k), ND[k] * MC - 1))
                step(na, folded[:], folded[:], acc[:, s, :, :].rearrange("p a o -> p (a o)"))
                pool.wait_ge(g_done, g_count(n - SLOTS))
                nc.gpsimd.tensor_tensor(x2[s][:], folded[:, 0:P], folded[:, P:2 * P], ALU.add).then_inc(x2_ready, 1)

            def blocks(t, first, end, ahead):
                for k in range(first, end):
                    if ahead and k == HEAD:
                        pool.wait_ge(turned, QUADS * (t + 1))
                        take_ids(t + 1)
                    if ahead:
                        for m in range(GATHERS * (k - HEAD), min(M, GATHERS * (k - HEAD + 1))):
                            gather(m)
                    sum_block(t, k)

            blocks(0, 0, HEAD, False)
            with pool.Fori(0, TILES - 1) as t:
                blocks(t, HEAD, BLOCKS, True)
                blocks(t + 1, 0, HEAD, False)
            blocks(TILES - 1, HEAD, BLOCKS, False)

        @block.tensor
        def _(pe):
            def transpose_part(t, i):
                if i == 0:
                    pe.wait_ge(gathered, 16 * M * (t + 1))
                    pe.wait_ge(ec_ready, QUADS * t)
                else:
                    pe.wait_ge(el_ready, QUADS * t + i)
                pe.sem_inc(turn_seen, 1)
                for dd in range(4):
                    ins = nc.tensor.transpose(rep_ps[0:M, dd * P:(dd + 1) * P],
                                              e[:].rearrange("p (m d) -> p d m", d=D)[:, 4 * i + dd, :], ident[:])
                ins.then_inc(turned, 1)

            def e_cols(q):
                return eT[:, q * QC:(q + 1) * QC]

            def first_factor(n, q):
                pe.wait_ge(el_ready, n - q + QUADS)
                if q == 0:
                    pe.wait_ge(ec_ready, n + 1)
                else:
                    pe.wait_ge(ec_ready, n)
                    pe.wait_ge(pair_ready, GROUPS * n)
                nc.tensor.matmul(rep_ps[0:GP, :], sel[:, GROUPS, :], e_cols(q), start=True, stop=True).then_inc(first_rep, 1)

            def scalars(n, q):
                if q == 0:
                    pe.wait_ge(el_ready, n + QUADS)
                else:
                    pe.wait_ge(pair_ready, GROUPS * (n + 1))
                for j in range(JB):
                    ins = nc.tensor.matmul(rep_ps[:, j * M:(j + 1) * M], eT[:, q * QC + j * P:q * QC + (j + 1) * P],
                                           unit[:], start=True, stop=True)
                ins.then_inc(scalars_rep, 1)

            def rep(n, q, g):
                if g == 0:
                    pe.wait_ge(first_ready, n + 1)
                else:
                    pe.wait_ge(pair_ready, GROUPS * n + g)
                nc.tensor.matmul(rep_ps[0:GP, :], sel[:, g, :], e_cols(q), start=True, stop=True).then_inc(rep_ready, 1)

            def layer1(n, g):
                pe.wait_ge(pair_ready, GROUPS * n + g + 1)
                if g == 0:
                    pe.wait_ge(z1_out, n)
                ins = nc.tensor.matmul(x1_ps[:], k0s[:, g, :], pairs[:, g, :], start=(g == 0), stop=(g == GROUPS - 1))
                if g == GROUPS - 1:
                    ins.then_inc(x1_done, 1)

            def layer2(t, k, u):
                s, j = (k // JB) % 2, k % JB
                if j == 0 and u == 0:
                    quad = t * QUADS + k // JB
                    pe.wait_ge(x1h_ready, quad + 1)
                    pe.wait_ge(x1l_ready, quad + 1)
                hi, lo = x1h[s][:, j * P:(j + 1) * P], x1l[s][:, j * P:(j + 1) * P]
                cols = slice(u * QC, (u + 1) * QC)
                if u in ACT_CHUNKS[k]:
                    a = ACT_CHUNKS[k].index(u)
                    pe.wait_ge(scaled_ready, scaled_count(act_chunk(t, k, a - YA)))
                    dst, ready = y_act[act_chunk(0, k, a) % YA], ya_ready
                else:
                    c = DVE_CHUNKS[k].index(u)
                    pe.wait_ge(acc_step, acc_count(dve_chunk(t, k, c - YD)))
                    dst, ready = y_dve[dve_chunk(0, k, c) % YD], yd_ready
                nc.tensor.matmul(dst[:], hi, k1h[:, cols], start=True, stop=False)
                nc.tensor.matmul(dst[:], hi, k1l[:, cols], start=False, stop=False)
                nc.tensor.matmul(dst[:], lo, k1h[:, cols], start=False, stop=True).then_inc(ready, 1)

            def gram(t, k):
                n = t * BLOCKS + k
                pe.wait_ge(x2_ready, x2_count(n))
                pe.wait_ge(ebd_ready, ONE + n + 1)
                pe.wait_ge(g_out, ONE + n)
                if k == 0:
                    pe.wait_ge(z3_out, ONE + t)
                nc.tensor.matmul(g_ps[:, 0:BB * M1], x2[k % 2][:], ebd[:].rearrange("p b m -> p (b m)"),
                                 start=True, stop=True).then_inc(g_done, 1)

            def layer3(t, part):
                if part == 0:
                    pe.wait_ge(g_out, ONE + (t + 1) * BLOCKS)
                size = M // len(L3_AT)
                for m in range(part * size, (part + 1) * size):
                    ins = nc.tensor.matmul(g_ps[:, 0:P], k2[:, m * P:(m + 1) * P], G[:, m, :],
                                           start=(m == 0), stop=(m == M - 1))
                if m == M - 1:
                    ins.then_inc(z3_done, 1)

            def blocks(t, first, end, after, ahead):
                for k in range(first, end):
                    n = t * QUADS + k // JB + 1
                    q = (k // JB + 1) % QUADS
                    for u in range(CHUNKS):
                        layer2(t, k, u)
                        if u == G_AT:
                            if k >= LAG:
                                gram(t, k - LAG)
                            elif after:
                                gram(t - 1, k - LAG + BLOCKS)
                        if after and k * CHUNKS + u in L3_AT:
                            layer3(t - 1, L3_AT[k * CHUNKS + u])
                        if q == 0 and not ahead:
                            continue
                        step = front_steps(k, u)
                        if "turn" in step:
                            transpose_part(t + 1, step["turn"])
                        if "first" in step:
                            first_factor(n, q)
                        if "scalars" in step:
                            scalars(n, q)
                        if "rep" in step:
                            rep(n, q, step["rep"])
                        if "layer1" in step:
                            layer1(n, step["layer1"])

            pe.sem_inc(g_done, SLOTS)
            pe.sem_inc(z3_done, ONE)
            pe.sem_inc(ya_ready, ONE)
            pe.wait_ge(const_ready, 1)
            pe.wait_ge(pool_const, 8)
            for i in range(4):
                transpose_part(0, i)
            scalars(0, 0)
            first_factor(0, 0)
            pe.wait_ge(k0_ready, 1)
            for g in range(GROUPS):
                rep(0, 0, g)
                if g >= 1:
                    layer1(0, g - 1)
            layer1(0, GROUPS - 1)
            pe.wait_ge(k1_ready, 1)
            pe.wait_ge(late_in, LATE)
            blocks(0, 0, HEAD, False, True)
            with pe.Fori(0, TILES - 1) as t:
                blocks(t, HEAD, BLOCKS, False, True)
                blocks(t + 1, 0, HEAD, True, True)
            blocks(TILES - 1, HEAD, BLOCKS, False, False)
            for k in range(BLOCKS - LAG, BLOCKS):
                gram(TILES - 1, k)
            for part in range(len(L3_AT)):
                layer3(TILES - 1, part)

            pe.wait_ge(z3_out, ONE + TILES)
            pe.wait_ge(z1_out, TILES * QUADS)
            done = 0
            for half in range(2):
                cols = slice(half * QC, (half + 1) * QC)
                for f in range(F1):
                    if half:
                        pe.wait_ge(mlp_out, done - len(mlp_banks) + 1)
                    ps = mlp_banks[done % len(mlp_banks)]
                    fs = slice(f * P, (f + 1) * P)
                    for i in range(3):
                        nc.tensor.matmul(ps[:], w1z[:, i, fs], z[i][:, cols], start=(i == 0), stop=False)
                    nc.tensor.matmul(ps[:], w1d[:, fs], dense[:, cols], start=False, stop=True).then_inc(mlp_done, 1)
                    done += 1
                for f in range(F2):
                    ps = mlp_banks[done % len(mlp_banks)]
                    for i in range(F1):
                        if f == 0:
                            pe.wait_ge(mlp_out, half * (F1 + F2 + 1) + i + 1)
                        ins = nc.tensor.matmul(ps[:], w2s[:, i, f * P:(f + 1) * P], h1[:, i, :],
                                               start=(i == 0), stop=(i == F1 - 1))
                    ins.then_inc(mlp_done, 1)
                    done += 1
                ps = mlp_banks[done % len(mlp_banks)]
                for i in range(F2):
                    pe.wait_ge(mlp_out, half * (F1 + F2 + 1) + F1 + i + 1)
                    ins = nc.tensor.matmul(ps[0:1, :], w3s[:, i:i + 1], h2[:, i, :], start=(i == 0), stop=(i == F2 - 1))
                ins.then_inc(mlp_done, 1)
                done += 1

        @block.scalar
        def _(act):
            def high_part(t, i):
                act.wait_ge(turned, QUADS * t + i + 1)
                if i == 0:
                    act.wait_ge(x1_done, QUADS * t)
                nc.scalar.copy(eT[0:M, :].rearrange("p (b d) -> p d b", d=D)[:, 4 * i:4 * i + 4, :],
                               rep_ps[0:M, :].rearrange("p (d b) -> p d b", d=4)).then_inc(eh_ready, 1)

            def take_first(n):
                act.wait_ge(first_rep, n + 1)
                act.wait_ge(pair_ready, GROUPS * n)
                nc.scalar.copy(first[:], rep_ps[0:GP, :]).then_inc(first_ready, 1)

            def take_scalars(n, q):
                act.wait_ge(scalars_rep, n + 1)
                if not (isinstance(n, int) and n == 0):
                    act.wait_ge(ebd_ready, ONE + JB * (n - 1))
                nc.scalar.copy(ec[q % 2][:, :, 0:M], rep_ps[:, 0:JB * M].rearrange("p (j m) -> p j m", j=JB))\
                    .then_inc(ec_ready, 1)

            def take_x1(n, q):
                act.wait_ge(x1_done, n + 1)
                nc.scalar.copy(x1h[q % 2][:], x1_ps[:]).then_inc(x1h_ready, 1)

            def scale_chunk(t, k, u):
                a = ACT_CHUNKS[k].index(u)
                q, j = k // JB, k % JB
                act.wait_ge(ya_ready, ONE + act_chunk(t, k, a) + 1)
                if j == 0 and a == 0:
                    act.wait_ge(ec_ready, t * QUADS + q + 1)
                if a == 0:
                    act.wait_ge(x2_ready, x2_count(t * BLOCKS + k - SLOTS))
                ps = y_act[act_chunk(0, k, a) % YA]
                for i in range(MC):
                    m = u * MC + i
                    ins = nc.scalar.activation(scaled[:, k % 2, a, i * P:(i + 1) * P], ps[:, i * P:(i + 1) * P], ACT.Copy,
                                               scale=ec[q % 2][:, j, m:m + 1])
                ins.then_inc(scaled_ready, 1)

            def take_gram(t, k):
                n = t * BLOCKS + k
                act.wait_ge(g_done, g_count(n))
                if k == 0:
                    act.wait_ge(z3_done, ONE + t)
                nc.scalar.copy(G[:, :, k * BB:(k + 1) * BB],
                               g_ps[:, 0:BB * M1].rearrange("p (b m) -> p m b", m=M1)).then_inc(g_out, 1)

            def samples(t):
                return slice(t * P, (t + 1) * P) if isinstance(t, int) else bass.ds(t * P, P)

            def take_z(t):
                act.wait_ge(g_out, ONE + (t + 1) * BLOCKS)
                nc.scalar.copy(z[1][:, samples(t)], G[:, M, :])
                act.wait_ge(z3_done, ONE + t + 1)
                nc.scalar.copy(z[2][:, samples(t)], g_ps[:, 0:P]).then_inc(z3_out, 1)

            def blocks(t, first, end, after, ahead):
                for k in range(first, end):
                    n = t * QUADS + k // JB + 1
                    q = (k // JB + 1) % QUADS
                    for u in range(CHUNKS):
                        if u in ACT_CHUNKS[k]:
                            scale_chunk(t, k, u)
                        if after and k * CHUNKS + u == max(L3_AT):
                            take_z(t - 1)
                        if u == G_AT + 1:
                            if k >= LAG:
                                take_gram(t, k - LAG)
                            elif after:
                                take_gram(t - 1, k - LAG + BLOCKS)
                        if q == 0 and not ahead:
                            continue
                        step = front_steps(k, u)
                        if "turn" in step:
                            high_part(t + 1, step["turn"])
                        if "first" in step:
                            take_first(n)
                        if "scalars" in step:
                            take_scalars(n, q)
                        if step.get("layer1") == GROUPS - 1:
                            take_x1(n, q)

            act.sem_inc(scaled_ready, YA)
            act.sem_inc(g_out, ONE)
            act.sem_inc(z3_out, ONE)
            act.wait_ge(const_ready, 1)
            for i in range(4):
                high_part(0, i)
            take_scalars(0, 0)
            take_first(0)
            take_x1(0, 0)
            blocks(0, 0, HEAD, False, True)
            with act.Fori(0, TILES - 1) as t:
                blocks(t, HEAD, BLOCKS, False, True)
                blocks(t + 1, 0, HEAD, True, True)
            blocks(TILES - 1, HEAD, BLOCKS, False, False)
            for k in range(BLOCKS - LAG, BLOCKS):
                take_gram(TILES - 1, k)
            take_z(TILES - 1)

            act.wait_ge(late_in, LATE)
            done = 0
            for half in range(2):
                for f in range(F1):
                    act.wait_ge(mlp_done, done + 1)
                    if half and f == 0:
                        act.wait_ge(mlp_done, F1 + F2 + 1)
                    nc.scalar.activation(h1[:, f, :], mlp_banks[done % len(mlp_banks)][:], ACT.Relu, bias=b1s[:, f:f + 1]).then_inc(mlp_out, 1)
                    done += 1
                for f in range(F2):
                    act.wait_ge(mlp_done, done + 1)
                    nc.scalar.activation(h2[:, f, :], mlp_banks[done % len(mlp_banks)][:], ACT.Relu, bias=b2s[:, f:f + 1]).then_inc(mlp_out, 1)
                    done += 1
                act.wait_ge(mlp_done, done + 1)
                nc.scalar.copy(y[:, half * QC:(half + 1) * QC], mlp_banks[done % len(mlp_banks)][0:1, :]).then_inc(mlp_out, 1)
                done += 1

        @block.vector
        def _(dve):
            def low_part(t, i):
                dve.wait_ge(eh_ready, QUADS * t + i + 1)
                hi = eT[0:M, :].rearrange("p (b d) -> p d b", d=D)[:, 4 * i:4 * i + 4, :].bitcast(F32)
                lo = eT[LO:KE, :].rearrange("p (b d) -> p d b", d=D)[:, 4 * i:4 * i + 4, :]
                nc.vector.tensor_tensor(lo, rep_ps[0:M, :].rearrange("p (d b) -> p d b", d=4), hi, ALU.subtract)\
                    .then_inc(el_ready, 1)

            def pair(n, g):
                dve.wait_ge(rep_ready, GROUPS * n + g + 1)
                if g == 0:
                    dve.wait_ge(first_ready, n + 1)
                    dve.wait_ge(x1_done, n)
                nc.vector.tensor_tensor(pairs[:, g, :], rep_ps[0:GP, :], first[:], ALU.mult).then_inc(pair_ready, 1)

            def take_x1(n, q, cols):
                dve.wait_ge(x1h_ready, n + 1)
                nc.vector.tensor_tensor(x1l[q % 2][:], x1_ps[:], x1h[q % 2][:].bitcast(F32), ALU.subtract)\
                    .then_inc(x1l_ready, 1)
                nc.vector.tensor_reduce(z[0][:, cols], x1_ps[:].rearrange("p (b d) -> p b d", d=D), AX.X, ALU.add)\
                    .then_inc(z1_out, 1)

            def sum_chunk(t, k, u):
                c = DVE_CHUNKS[k].index(u)
                q, j = k // JB, k % JB
                dve.wait_ge(yd_ready, dve_chunk(t, k, c) + 1)
                if j == 0 and c == 0:
                    dve.wait_ge(ec_ready, t * QUADS + q + 1)
                if c == 0:
                    dve.wait_ge(x2_ready, x2_count(t * BLOCKS + k - SLOTS))
                ps = y_dve[dve_chunk(0, k, c) % YD]
                for i in range(MC):
                    m, step = u * MC + i, c * MC + i
                    into = acc[:, k % 2, step % 2, :]
                    scalar = ec[q % 2][:, j, m:m + 1]
                    if step < 2:
                        ins = nc.vector.tensor_scalar(into, ps[:, i * P:(i + 1) * P], scalar, None, ALU.mult)
                    else:
                        dve.wait_ge(acc_step, acc_count(dve_chunk(t, k), step - 2))
                        ins = nc.vector.scalar_tensor_tensor(out=into, in0=ps[:, i * P:(i + 1) * P], scalar=scalar,
                                                             in1=into, op0=ALU.mult, op1=ALU.add)
                    ins.then_inc(acc_step, 1)

            def diagonal(t, k):
                n = t * BLOCKS + k
                q, j = k // JB, k % JB
                dve.wait_ge(g_done, g_count(n - 1))
                nc.vector.tensor_tensor(ebd[:], ec[q % 2][:, j:j + 1, :].to_broadcast([P, BB, M1]),
                                        mask[:].rearrange("p (b a) -> p b a", a=1).to_broadcast([P, BB, M1]), ALU.mult)\
                    .then_inc(ebd_ready, 1)

            def blocks(t, first, end, after, ahead):
                for k in range(first, end):
                    n = t * QUADS + k // JB + 1
                    q = (k // JB + 1) % QUADS
                    if k >= LAG:
                        diagonal(t, k - LAG)
                    elif after:
                        diagonal(t - 1, k - LAG + BLOCKS)
                    for u in range(CHUNKS):
                        if u in DVE_CHUNKS[k]:
                            sum_chunk(t, k, u)
                        if q == 0 and not ahead:
                            continue
                        step = front_steps(k, u)
                        if "turn" in step:
                            low_part(t + 1, step["turn"])
                        if "rep" in step:
                            pair(n, step["rep"])
                        if step.get("layer1") == GROUPS - 1:
                            take_x1(n, q, bass.ds(n * QB, QB) if not isinstance(n, int) else slice(n * QB, (n + 1) * QB))

            dve.sem_inc(acc_step, YD * MC)
            dve.sem_inc(ebd_ready, ONE)
            nc.vector.memset(eT[32:LO, :].bitcast(F32), 0.0)
            for i in range(2):
                nc.vector.memset(ec[i][:, :, M:M1], 1.0)
            dve.wait_ge(k1_in, 16)
            nc.vector.tensor_copy(k1h[:], k1_raw).then_inc(k1_ready, 1)
            dve.wait_ge(k1_ready, 1)
            nc.vector.tensor_tensor(k1l[:], k1_raw, k1h[:].bitcast(F32), ALU.subtract)
            dve.wait_ge(k0_in, 32)
            nc.vector.tensor_tensor(k0s[0:2 * M, 0:2, :], k0s[0:2 * M, 0:2, :], k0b[0:2 * M, 0:2, :], ALU.add)
            nc.vector.tensor_tensor(k0s[:, 2:, :], k0s[:, 2:, :], k0b[:, 2:, :], ALU.add).then_inc(k0_ready, 1)
            dve.wait_ge(pool_const, 8)
            for g in range(GROUPS):
                for a in range(3):
                    s = SHIFTS[g][a]
                    nc.vector.tensor_copy(sel[:, g, a * M:(a + 1) * M], shifted[:, s:s + M])
            for a in range(3):
                nc.vector.tensor_copy(sel[:, GROUPS, a * M:(a + 1) * M], shifted[:, 0:M])
            nc.vector.tensor_copy(unit[:], shifted[:, 0:M]).then_inc(const_ready, 1)
            for i in range(4):
                low_part(0, i)
            for g in range(GROUPS):
                pair(0, g)
            take_x1(0, 0, slice(0, QB))
            blocks(0, 0, HEAD, False, True)
            with dve.Fori(0, TILES - 1) as t:
                blocks(t, HEAD, BLOCKS, False, True)
                blocks(t + 1, 0, HEAD, True, True)
            blocks(TILES - 1, HEAD, BLOCKS, False, False)
            for k in range(BLOCKS - LAG, BLOCKS):
                diagonal(TILES - 1, k)


def kernel(**inputs):
    import numpy as np
    import concourse.bacc as bacc
    from concourse.bass_utils import run_bass_kernel_spmd

    a = {k: np.asarray(v) for k, v in inputs.items()}
    tables = [a[f"tbl_{m}"] for m in range(M)]
    k0, k1, k2 = a["L0_rec_k0"], a["L0_rec_k1"], a["L0_rec_k2"]
    m = np.arange(M)
    pair = np.array([[(m + s) % M for s in group] for group in SHIFTS])
    own = np.broadcast_to(m, pair.shape)
    k0_first = k0[:, own, pair].transpose(2, 3, 1, 0).reshape(GP, GROUPS, P)
    k0_second = k0[:, pair, own].transpose(2, 3, 1, 0).reshape(GP, GROUPS, P)
    H1, H2 = a["W_top2"].shape
    arrays = {
        "dense_t": a["dense_ctx"].T, "ids": a["ids"],
        **{f"tbl_{i}": v for i, v in enumerate(tables)},
        "w1": a["W_top1"], "b1": a["b_top1"].reshape(H1 // P, P).T, "w2": a["W_top2"],
        "b2": a["b_top2"].reshape(H2 // P, P).T, "w3": a["W_top3"].reshape(H2 // P, P).T,
        "k0_first": k0_first, "k0_second": k0_second,
        "k1_t": k1.transpose(1, 2, 0).reshape(P, M * P), "k2_t": k2.transpose(1, 2, 0).reshape(P, M * P),
    }
    arrays = {k: np.ascontiguousarray(v) for k, v in arrays.items()}
    nc = bacc.Bacc("TRN2", target_bir_lowering=False, num_devices=1)
    ap = {k: nc.dram_tensor("in_" + k, v.shape, mybir.dt.from_np(v.dtype), kind="ExternalInput").ap()
          for k, v in arrays.items()}
    B = a["ids"].shape[0]
    out = nc.dram_tensor("out_y", (1, B), F32, kind="ExternalOutput").ap()
    cin_tower(nc, ap["dense_t"], ap["ids"], [ap[f"tbl_{i}"] for i in range(M)], ap["w1"], ap["b1"], ap["w2"], ap["b2"],
              ap["w3"], ap["k0_first"], ap["k0_second"], ap["k1_t"], ap["k2_t"], out)
    r = run_bass_kernel_spmd(nc, [{"in_" + k: v for k, v in arrays.items()}], core_ids=[0])
    return r.results[0]["out_y"].reshape(B, 1)
```

```python
from contextlib import ExitStack

import concourse.bass as bass
from concourse import mybir

F32 = mybir.dt.float32
F32R = mybir.dt.float32r
I32 = mybir.dt.int32
ALU = mybir.AluOpType
ACT = mybir.ActivationFunctionType
AX = mybir.AxisListType

P = 128
M, D = 40, 16
QC = 512
QB = QC // D
BB = P // D
QUADS = P // QB
JB = QC // P
BLOCKS = P // BB
MC = QC // P
CHUNKS = M // MC
M1 = M + 1

SPLIT = 5
RING = 3
SHIFTS = [(1, 2, 0), (3, 4, M // 2)] + [(s, s + 1, s + 2) for s in range(5, M // 2, 3)]
GROUPS = len(SHIFTS)
GP = 3 * M
FIRST = GROUPS
LOADS = [(FIRST, 1, 0, 3, 0, 0), (0, 1, 0, 2, 1, 1), (0, 1, 2, 1, 0, 1), (1, 1, 0, 2, 3, 1), (1, 1, 2, 1, M // 2, 1),
         *((2, GROUPS - 2, a, 1, 5 + a, 1) for a in range(3))]

SHARES = {4: (1, 4, 6, 9), 5: (1, 3, 5, 7, 9), 6: (0, 2, 4, 6, 8, 9)}
NA = [4, 4, 4, 4, 4, 4, 5, 5, 5, 4, 4, 4, 4, 4, 4, 5]
ACT_CHUNKS = [SHARES[n] for n in NA]
DVE_CHUNKS = [tuple(u for u in range(CHUNKS) if u not in c) for c in ACT_CHUNKS]
ND = [CHUNKS - n for n in NA]
NA_TILE, ND_TILE = sum(NA), sum(ND)
YA, YD = 2, 4
assert len(NA) == BLOCKS and NA_TILE % YA == 0 and ND_TILE % YD == 0
LAG = 2
G_AT = 8
X2_AT = 3
HEAD = LAG + 1

PAIR_AT = (-18, -15, -6, 0, 6, 12, 18)
HIGH_AT = (-13, -10, -1, 5, 11)
LOW_AT = (-8, -3, 3, 9, 15)
L1_AT = (1, 5, 9, 15, 21, 23, 25)
STEPS = {"scalars": (1,), "x1_high": (26,), "x1_low": (29,),
         "pair": PAIR_AT, "high": HIGH_AT, "low": LOW_AT, "layer1": L1_AT}
TURN_QUAD, TURN_AT = 2, (2, 3, 5, 6)
L3_AT = {21 + i: i for i in range(5)}

TURNED_IN = 9
GATHERED_IN = 6


def gathers_of(k):
    late = BLOCKS - TURNED_IN
    at = k - TURNED_IN if k >= TURNED_IN else min(k, GATHERED_IN) + late
    end = at + (k >= TURNED_IN or k < GATHERED_IN)
    return list(range(M * at // (late + GATHERED_IN), M * end // (late + GATHERED_IN)))


def front_steps(k, u):
    at = (k % JB) * CHUNKS + u
    steps = [(name, i, k // JB + ahead) for name, slots in STEPS.items() for i, slot in enumerate(slots)
             for ahead in (1, 2) if slot == at - (ahead - 1) * JB * CHUNKS]
    if k // JB == TURN_QUAD and at in TURN_AT:
        steps.append(("turn", TURN_AT.index(at), QUADS))
    return steps


def cin_tower(nc, e_rows, dense_t, ids, tables, w1, b1, w2, b2, w3, k0_first, k0_second, k1_t, k2_t, out):
    B = ids.shape[0]
    TILES = B // P
    H1, H2 = w1.shape[1], w2.shape[1]
    F1, F2 = H1 // P, H2 // P
    DC = dense_t.shape[0]

    with ExitStack() as ctx:
        def sb(name, shape, dt=F32):
            return ctx.enter_context(nc.sbuf_tensor(name, shape, dt))

        def shared(name, shape):
            with nc.sbuf_tensor(name, shape, F32) as tensor:
                pass
            return tensor, sb(name + "_late", shape, F32R)

        def sem(name):
            return ctx.enter_context(nc.semaphore(name))

        ids_all = sb("ids_all", [P, TILES, M], I32)
        ids_now = sb("ids_now", [P, M], I32)
        e = sb("e", [P, M * D])
        eT = sb("eT", [M, P * D])
        rotated = [sb(f"rotated{i}", [P, GROUPS + 1, QC]) for i in range(2)]
        pair_hi = [sb(f"pair_hi{i}", [GP, QC], F32R) for i in range(RING)]
        pair_lo = [sb(f"pair_lo{i}", [GP, QC], F32R) for i in range(RING)]
        k0s = sb("k0s", [GP, GROUPS, P])
        k0h = sb("k0h", [GP, SPLIT, P], F32R)
        k0l = sb("k0l", [GP, SPLIT, P], F32R)
        x1h = [sb(f"x1h{i}", [P, QC], F32R) for i in range(2)]
        x1l = [sb(f"x1l{i}", [P, QC], F32R) for i in range(2)]
        ec = [sb(f"ec{i}", [P, JB, M]) for i in range(QUADS)]
        k1h = sb("k1h", [P, M * P], F32R)
        k1l = sb("k1l", [P, M * P], F32R)
        k2, k2_late = shared("k2", [P, M * P])
        scaled, scaled_late = shared("scaled", [P, 2, max(NA), QC])
        k0b = scaled[0:GP, 0, 0:2, :].rearrange("p a b -> p (a b)")[:, 0:GROUPS * P]\
            .rearrange("p (g o) -> p g o", g=GROUPS)
        acc = sb("acc", [P, 2, 2, P])
        sums = sb("sums", [P, QC])
        folded = sb("folded", [P, 2, 2 * P])
        fold = sb("fold", [P, 2 * P])
        x2 = [sb(f"x2{i}", [P, P]) for i in range(2)]
        mask = sb("mask", [P, BB])
        ebd = [sb(f"ebd{i}", [P, JB, BB, M1]) for i in range(2)]
        G = sb("G", [P, M1, P])
        k1_raw = G[:, 0:M, :].rearrange("p m o -> p (m o)")
        ident = sb("ident", [P, P])
        z = [sb(f"z{i}", [P, B]) for i in range(3)]
        late = rotated[0][:].rearrange("p g c -> p (g c)")
        w1z = late[:, 0:3 * H1].rearrange("p (k n) -> p k n", k=3)
        w2s = late[:, 3 * H1:3 * H1 + F1 * H2].rearrange("p (k n) -> p k n", k=F1)
        w1d = late[0:DC, 3 * H1 + F1 * H2:4 * H1 + F1 * H2]
        dense = late[0:DC, 4 * H1 + F1 * H2:4 * H1 + F1 * H2 + B]
        w1z_flat, w2_flat = late[:, 0:3 * H1], late[:, 3 * H1:3 * H1 + F1 * H2]
        w3s = sb("w3s", [P, F2])
        b1s = sb("b1s", [P, F1])
        b2s = sb("b2s", [P, F2])

        def mlp_operands(k1_part):
            sizes = (3 * H1, F1 * H2, F2, H1, B)
            ends = [sum(sizes[:n + 1]) for n in range(len(sizes))]
            rows = (P, P, P, DC, DC)
            return [k1_part[0:p, end - size:end] for p, size, end in zip(rows, sizes, ends)]

        operands = [w1z_flat, w2_flat, w3s[:], w1d, dense]
        operands_hi, operands_lo = mlp_operands(k1h), mlp_operands(k1l)

        def slots(buffer):
            return [buffer[:, first:first + QC] for first in range(0, buffer.shape[1], QC)]

        free = [*slots(scaled_late[:].rearrange("p s a c -> p (s a c)")),
                x1h[0][:], x1h[1][:], x1l[0][:], x1l[1][:], *slots(k2_late[:])]
        z_hi, z_lo = ([free[6 * half + 3 * part:6 * half + 3 * part + 3] for half in range(2)] for part in range(2))
        h_hi, h_lo = ([free[12 + 6 * part:12 + 6 * part + F1], free[12 + 6 * part + F1:12 + 6 * part + F1 + F2]]
                      for part in range(2))
        G_flat = G[:].rearrange("p m b -> p (m b)")
        relu = [G_flat[:, (F1 + F2 + n) * QC:(F1 + F2 + n + 1) * QC] for n in range(3)]
        hidden = (F1, F2, 1)
        JOBS = [(half, layer, f) for half, layer in ((0, 0), (0, 1), (1, 0), (0, 2), (1, 1), (1, 2))
                for f in range(hidden[layer])]
        PARTS = [job for job in JOBS if job[1] < 2]
        y = eT[0:1, 0:B]

        def bank(name):
            return ctx.enter_context(nc.psum_tensor(name, [P, QC], F32))

        y_act = [bank(f"y_act{i}") for i in range(YA)]
        y_dve = [bank(f"y_dve{i}") for i in range(YD)]
        x1_ps, g_ps = bank("x1_ps"), bank("g_ps")


        def turn_ps(t, i):
            return x1_ps if isinstance(t, int) and i % 2 else g_ps

        mlp_banks = [*y_act, *y_dve, x1_ps]

        ids_in, k0_in, k1_in, k2_in, late_in = sem("ids_in"), sem("k0_in"), sem("k1_in"), sem("k2_in"), sem("late_in")
        placed = [sem(f"placed{i}") for i in range(2)]
        gathered, out_done = sem("gathered"), sem("out_done")
        rows_stored, quad_stored = sem("rows_stored"), sem("quad_stored")
        rotated_in = [[sem(f"rotated_in{i}{j}") for j in range(2)] for i in range(2)]
        pool_const, k0_ready, k1_ready = sem("pool_const"), sem("k0_ready"), sem("k1_ready")
        ids_ready, ids_seen, turn_seen = sem("ids_ready"), sem("ids_seen"), sem("turn_seen")
        turned, scalars_turned, l1_step = sem("turned"), sem("scalars_turned"), sem("l1_step")
        ya_ready, yd_ready, g_done, z3_done, mlp_done = (
            sem("ya_ready"), sem("yd_ready"), sem("g_done"), sem("z3_done"), sem("mlp_done"))
        eT_ready, ec_ready, hi_ready, x1h_ready = sem("eT_ready"), sem("ec_ready"), sem("hi_ready"), sem("x1h_ready")
        scaled_ready, g_out, z3_out, mlp_out = sem("scaled_ready"), sem("g_out"), sem("z3_out"), sem("mlp_out")
        split_high, split_low, h_high, h_low = sem("split_high"), sem("split_low"), sem("h_high"), sem("h_low")
        pair_ready, lo_ready, x1l_ready, z1_out = sem("pair_ready"), sem("lo_ready"), sem("x1l_ready"), sem("z1_out")
        acc_step, x2_ready, ebd_cleared = sem("acc_step"), sem("x2_ready"), sem("ebd_cleared")
        sum_step, folded_ready = sem("sum_step"), sem("folded_ready")

        SLOTS = 2

        def act_chunk(t, k, a=0):
            return t * NA_TILE + sum(NA[:k]) + a

        def dve_chunk(t, k, c=0):
            return t * ND_TILE + sum(ND[:k]) + c

        def scaled_count(chunk):
            return chunk + 1 + YA

        def acc_count(chunk, step=MC - 1):
            return (chunk + YD) * MC + step + 1

        def folded_count(n):
            return n + 1 + SLOTS

        def x2_count(n):
            return n + 1 + SLOTS

        def g_count(n):
            return n + 1 + SLOTS * JB

        ONE = 1

        block = ctx.enter_context(nc.Block())

        @block.sync
        def _(sp):
            sp.dma_start(ids_all[:], ids.rearrange("(t p) m -> p t m", p=P)).then_inc(ids_in, 16)
            sp.dma_start(k0s[:], k0_first).then_inc(k0_in, 16)
            sp.dma_start(k0b[:], k0_second).then_inc(k0_in, 16)
            sp.dma_start(k1_raw, k1_t).then_inc(k1_in, 16)
            sp.dma_start(k2[:], k2_t).then_inc(k2_in, 16)
            sp.dma_start(w3s[:], w3).then_inc(late_in, 16)
            sp.dma_start(b1s[:], b1).then_inc(late_in, 16)
            sp.dma_start(b2s[:], b2).then_inc(late_in, 16)

            def store_rows(t, cols, stored):
                sp.wait_ge(eT_ready, QUADS * (t + 1))
                first = t * 2 * M
                dst = e_rows[first:first + M, cols] if isinstance(t, int) else e_rows[bass.ds(first, M), cols]
                (down, _), (across, width) = dst.ap
                dst = bass.AP(tensor=dst.tensor, offset=dst.offset, ap=[[down, M], [M * down, 2], [across, width]])
                src = eT[:, cols].rearrange("p (a c) -> p a c", a=1).to_broadcast([M, 2, width])
                sp.dma_start(dst, src).then_inc(stored, 16)

            def load_rotated(t, q):
                n = t * QUADS + q
                if not (isinstance(n, int) and n < 2):
                    sp.wait_ge(l1_step, GROUPS * (n - 1))
                cols = slice(q * QC, (q + 1) * QC)
                for g, groups, a, count, shift, step in LOADS:
                    row = t * 2 * M + shift
                    rows = e_rows[row:row + M, cols] if isinstance(row, int) else e_rows[bass.ds(row, M), cols]
                    (down, _), (across, _) = rows.ap
                    src = bass.AP(tensor=rows.tensor, offset=rows.offset,
                                  ap=[[step * down, count], [down, M], [across, QC]] if groups == 1 else
                                     [[down, M], [3 * down, groups], [across, QC]])
                    sp.dma_start(rotated[q % 2][a * M:(a + count) * M, g:g + groups, :], src)\
                        .then_inc(rotated_in[q % 2][groups > 1], 16)

            def place_diagonal(t, q):
                n = t * QUADS + q
                sp.wait_ge(ec_ready, n + 1)
                sp.wait_ge(g_done, g_count(JB * (n - 1) - 1))
                for b in range(BB):
                    rows = slice(b * D, (b + 1) * D)
                    sp.dma_start(ebd[q % 2][rows, :, b, 0:M], ec[q][rows, :, :]).then_inc(placed[q % 2], 16)

            store_rows(0, slice(0, QC), quad_stored)
            store_rows(0, slice(QC, P * D), rows_stored)
            sp.wait_ge(quad_stored, 16)
            load_rotated(0, 0)
            sp.wait_ge(rows_stored, 16)
            load_rotated(0, 1)
            sp.wait_ge(ebd_cleared, 1)
            place_diagonal(0, 0)
            load_rotated(0, 2)
            with sp.Fori(0, TILES - 1) as t:
                place_diagonal(t, 1)
                load_rotated(t, 3)
                place_diagonal(t, 2)
                store_rows(t + 1, slice(0, P * D), rows_stored)
                sp.wait_ge(rows_stored, 16 * (t + 2))
                load_rotated(t + 1, 0)
                place_diagonal(t, 3)
                load_rotated(t + 1, 1)
                place_diagonal(t + 1, 0)
                load_rotated(t + 1, 2)
            place_diagonal(TILES - 1, 1)
            load_rotated(TILES - 1, 3)
            place_diagonal(TILES - 1, 2)
            place_diagonal(TILES - 1, 3)
            sp.wait_ge(l1_step, GROUPS * TILES * QUADS)
            sp.dma_start(w1z, w1[0:3 * P, :].rearrange("(k p) n -> p k n", p=P)).then_inc(late_in, 16)
            sp.dma_start(w1d, w1[3 * P:3 * P + DC, :]).then_inc(late_in, 16)
            sp.dma_start(w2s, w2.rearrange("(k p) n -> p k n", p=P)).then_inc(late_in, 16)
            sp.dma_start(dense, dense_t).then_inc(late_in, 16)
            sp.wait_ge(mlp_out, len(JOBS))
            sp.dma_start(out, y).then_inc(out_done, 16)
            sp.wait_ge(out_done, 16)
        LATE = 7 * 16
        SPLITS_OF_HALF = (len(operands_hi) + 3, len(operands_hi) + 6)

        @block.gpsimd
        def _(pool):
            def take_ids(t):
                if not (isinstance(t, int) and t == 0):
                    pool.wait_ge(gathered, 16 * M * t)
                nc.gpsimd.tensor_copy(ids_now[:], ids_all[:, t, :] if isinstance(t, int) else
                                      ids_all[:, bass.ds(t, 1), :].rearrange("p a m -> p (a m)")).then_inc(ids_ready, 1)
                pool.wait_ge(ids_ready, t + 1)
                pool.sem_inc(ids_seen, 1)

            def gather(m):
                pool.indirect_dma_start(e[:, m * D:(m + 1) * D], None, tables[m],
                                        bass.IndirectOffsetOnAxis(ap=ids_now[:, m:m + 1], axis=0)).then_inc(gathered, 16)

            pool.sem_inc(folded_ready, SLOTS)
            pool.wait_ge(ids_in, 16)
            take_ids(0)
            for m in range(M):
                gather(m)
            nc.gpsimd.memset(mask[:], 1.0).then_inc(pool_const, 1)
            nc.gpsimd.memset(ident[:], 0.0).then_inc(pool_const, 1)
            pool.wait_ge(pool_const, 2)
            nc.gpsimd.affine_select(out=ident[:], in_=ident[:], compare_op=ALU.not_equal, fill=1.0, base=0,
                                    pattern=[[-1, P]], channel_multiplier=1).then_inc(pool_const, 1)
            nc.gpsimd.affine_select(out=mask[:], in_=mask[:], compare_op=ALU.is_ge, fill=0.0, base=0,
                                    pattern=[[-D, BB]], channel_multiplier=1).then_inc(pool_const, 1)
            pool.wait_ge(pool_const, 4)
            nc.gpsimd.affine_select(out=mask[:], in_=mask[:], compare_op=ALU.is_ge, fill=0.0, base=D - 1,
                                    pattern=[[D, BB]], channel_multiplier=-1).then_inc(pool_const, 1)

            def sum_block(t, k, gathers):
                n = t * BLOCKS + k
                s, na = k % 2, NA[k]
                src = [scaled[:, s, a, :] for a in range(na)]
                before = t * NA_TILE + sum(NA[:k])

                def step(i, dst, a, b):
                    nc.gpsimd.tensor_tensor(dst, a, b, ALU.add).then_inc(sum_step, 1)
                    if gathers:
                        gather(gathers.pop(0))
                    pool.wait_ge(sum_step, before + i + 1)

                pool.wait_ge(scaled_ready, scaled_count(act_chunk(t, k, 1)))
                step(0, sums[:], src[0], src[1])
                for a in range(2, na):
                    pool.wait_ge(scaled_ready, scaled_count(act_chunk(t, k, a)))
                    step(a - 1, sums[:], sums[:], src[a])
                step(na - 1, fold[:], sums[:, 0:2 * P], sums[:, 2 * P:4 * P])
                pool.wait_ge(acc_step, acc_count(dve_chunk(t, k), ND[k] * MC - 1))
                pool.wait_ge(x2_ready, x2_count(n - SLOTS))
                nc.gpsimd.tensor_tensor(folded[:, s, :], fold[:], acc[:, s, :, :].rearrange("p a o -> p (a o)"), ALU.add)\
                    .then_inc(folded_ready, 1)

            def tile_body(t, ahead, far_ahead):
                for k in range(BLOCKS):
                    if k == TURNED_IN and far_ahead:
                        pool.wait_ge(turned, QUADS * (t + 2))
                        take_ids(t + 2)
                    sum_block(t, k, gathers_of(k) if (far_ahead if k >= TURNED_IN else ahead) else [])

            pool.wait_ge(turned, QUADS)
            take_ids(1)
            for k in range(TURNED_IN, BLOCKS):
                for m in gathers_of(k):
                    gather(m)
            with pool.Fori(0, TILES - 2) as t:
                tile_body(t, True, True)
            tile_body(TILES - 2, True, False)
            tile_body(TILES - 1, False, False)

        @block.tensor
        def _(pe):
            def transpose_part(t, i):
                if i == 0:
                    pe.wait_ge(gathered, 16 * M * (t + 1))
                    pe.wait_ge(ec_ready, QUADS * t)
                elif not isinstance(t, int):
                    pe.wait_ge(eT_ready, QUADS * t + i)
                elif i > 1:
                    pe.wait_ge(eT_ready, i - 1)
                pe.sem_inc(turn_seen, 1)
                for dd in range(4):
                    ins = nc.tensor.transpose(turn_ps(t, i)[0:M, dd * P:(dd + 1) * P],
                                              e[:].rearrange("p (m d) -> p d m", d=D)[:, 4 * i + dd, :], ident[:])
                ins.then_inc(turned, 1)

            def scalars(n, q, grams=None):
                if q == 0:
                    pe.wait_ge(eT_ready, n + QUADS)
                if grams is not None:
                    pe.wait_ge(g_out, ONE + grams)
                pe.sem_inc(turn_seen, 1)
                for j in range(JB):
                    ins = nc.tensor.transpose(g_ps[:, j * M:(j + 1) * M], eT[:, q * QC + j * P:q * QC + (j + 1) * P],
                                              ident[0:M, 0:M])
                ins.then_inc(scalars_turned, 1)

            def layer1(n, q, g):
                if g < SPLIT:
                    pe.wait_ge(lo_ready, SPLIT * n + g + 1)
                else:
                    pe.wait_ge(pair_ready, GROUPS * n + g + 1)
                if g == 0:
                    pe.wait_ge(z1_out, n)
                if g < SPLIT:
                    nc.tensor.matmul(x1_ps[:], k0h[:, g, :], pair_hi[g % RING][:], start=(g == 0), stop=False)
                    nc.tensor.matmul(x1_ps[:], k0l[:, g, :], pair_hi[g % RING][:], start=False, stop=False)
                    ins = nc.tensor.matmul(x1_ps[:], k0h[:, g, :], pair_lo[g % RING][:], start=False, stop=False)
                else:
                    ins = nc.tensor.matmul(x1_ps[:], k0s[:, g, :], rotated[q % 2][0:GP, g, :],
                                           start=(g == 0), stop=(g == GROUPS - 1))
                ins.then_inc(l1_step, 1)

            def layer2(t, k, u):
                s, j = (k // JB) % 2, k % JB
                if j == 0 and u == 0:
                    quad = t * QUADS + k // JB
                    pe.wait_ge(x1h_ready, quad + 1)
                    pe.wait_ge(x1l_ready, quad + 1)
                hi, lo = x1h[s][:, j * P:(j + 1) * P], x1l[s][:, j * P:(j + 1) * P]
                cols = slice(u * QC, (u + 1) * QC)
                if u in ACT_CHUNKS[k]:
                    a = ACT_CHUNKS[k].index(u)
                    pe.wait_ge(scaled_ready, scaled_count(act_chunk(t, k, a - YA)))
                    dst, ready = y_act[act_chunk(0, k, a) % YA], ya_ready
                else:
                    c = DVE_CHUNKS[k].index(u)
                    pe.wait_ge(acc_step, acc_count(dve_chunk(t, k, c - YD)))
                    dst, ready = y_dve[dve_chunk(0, k, c) % YD], yd_ready
                nc.tensor.matmul(dst[:], hi, k1h[:, cols], start=True, stop=False)
                nc.tensor.matmul(dst[:], hi, k1l[:, cols], start=False, stop=False)
                nc.tensor.matmul(dst[:], lo, k1h[:, cols], start=False, stop=True).then_inc(ready, 1)

            def gram(t, k, ec_count=None, eT_count=None):
                n = t * BLOCKS + k
                pe.wait_ge(x2_ready, x2_count(n))
                q = k // JB
                if k % JB == 0:
                    pe.wait_ge(placed[q % 2], 16 * BB * (t * QUADS // 2 + q // 2 + 1))
                pe.wait_ge(g_out, ONE + n)
                if ec_count is not None:
                    pe.wait_ge(ec_ready, ec_count)
                if eT_count is not None:
                    pe.wait_ge(eT_ready, eT_count)
                if k == 0:
                    pe.wait_ge(z3_out, ONE + t)
                nc.tensor.matmul(g_ps[:, 0:BB * M1], x2[k % 2][:], ebd[q % 2][:, k % JB, :, :].rearrange("p b m -> p (b m)"),
                                 start=True, stop=True).then_inc(g_done, 1)

            def layer3(t, part):
                if part == 0:
                    pe.wait_ge(g_out, ONE + (t + 1) * BLOCKS)
                size = M // len(L3_AT)
                for m in range(part * size, (part + 1) * size):
                    ins = nc.tensor.matmul(g_ps[:, 0:P], k2[:, m * P:(m + 1) * P], G[:, m, :],
                                           start=(m == 0), stop=(m == M - 1))
                if m == M - 1:
                    ins.then_inc(z3_done, 1)

            def front(name, i, n, q, t, grams):
                if name == "turn":
                    transpose_part(t + 1, i)
                elif name == "scalars":
                    scalars(n, q, grams)
                elif name == "layer1":
                    layer1(n, q, i)

            def blocks(t, first, end, after, ahead):
                for k in range(first, end):
                    for u in range(CHUNKS):
                        layer2(t, k, u)
                        if u == G_AT:
                            fronts = k % JB == 0 and (k // JB < QUADS - 1 or ahead)
                            ec_count = t * QUADS + k // JB + 2 if fronts else None
                            eT_count = QUADS * (t + 2) if fronts and k // JB == TURN_QUAD and ahead else None
                            if k >= LAG:
                                gram(t, k - LAG, ec_count, eT_count)
                            elif after:
                                gram(t - 1, k - LAG + BLOCKS, ec_count, eT_count)
                        if after and k * CHUNKS + u in L3_AT:
                            layer3(t - 1, L3_AT[k * CHUNKS + u])
                        for name, i, ahead_q in front_steps(k, u):
                            if ahead_q >= QUADS and not ahead:
                                continue
                            front(name, i, t * QUADS + ahead_q, ahead_q % QUADS, t,
                                  t * BLOCKS + k - LAG if k >= LAG or after else None)

            pe.sem_inc(g_done, SLOTS * JB)
            pe.sem_inc(z3_done, ONE)
            pe.sem_inc(ya_ready, ONE)
            pe.wait_ge(pool_const, 5)
            for i in range(4):
                transpose_part(0, i)
            scalars(0, 0)
            pe.wait_ge(k0_ready, 3)
            for g in range(GROUPS):
                layer1(0, 0, g)
            pe.wait_ge(k1_ready, 1)
            pe.wait_ge(k2_in, 16)
            blocks(0, 0, HEAD, False, True)
            with pe.Fori(0, TILES - 1) as t:
                blocks(t, HEAD, BLOCKS, False, True)
                blocks(t + 1, 0, HEAD, True, True)
            blocks(TILES - 1, HEAD, BLOCKS, False, False)
            for k in range(BLOCKS - LAG, BLOCKS):
                gram(TILES - 1, k)
            for part in range(len(L3_AT)):
                layer3(TILES - 1, part)

            (w1h, w2h, w3h, w1dh, dense_h), (w1l, w2l, w3l, w1dl, dense_l) = operands_hi, operands_lo
            for done, (half, layer, f) in enumerate(JOBS):
                if done >= len(mlp_banks):
                    pe.wait_ge(mlp_out, done - len(mlp_banks) + 1)
                ps = mlp_banks[done % len(mlp_banks)][0:P if layer < 2 else 1, :]
                if layer == 0:
                    pe.wait_ge(split_low, SPLITS_OF_HALF[half])
                    cols = slice(half * QC, (half + 1) * QC)
                    factors = [(w1h[:, i * H1 + f * P:i * H1 + (f + 1) * P], w1l[:, i * H1 + f * P:i * H1 + (f + 1) * P],
                                z_hi[half][i], z_lo[half][i]) for i in range(3)]
                    factors.append((w1dh[:, f * P:(f + 1) * P], w1dl[:, f * P:(f + 1) * P],
                                    dense_h[:, cols], dense_l[:, cols]))
                else:
                    wh, wl, size = (w2h, w2l, H2) if layer == 1 else (w3h, w3l, 1)
                    width = min(P, size)
                    factors = [(wh[:, i * size + f * width:i * size + (f + 1) * width],
                                wl[:, i * size + f * width:i * size + (f + 1) * width],
                                h_hi[layer - 1][i], h_lo[layer - 1][i]) for i in range(hidden[layer - 1])]
                for i, (wh_i, wl_i, in_hi, in_lo) in enumerate(factors):
                    if layer and f == 0:
                        pe.wait_ge(h_low, PARTS.index((half, layer - 1, i)) + 1)
                    nc.tensor.matmul(ps, wh_i, in_hi, start=(i == 0), stop=False)
                    nc.tensor.matmul(ps, wl_i, in_hi, start=False, stop=False)
                    ins = nc.tensor.matmul(ps, wh_i, in_lo, start=False, stop=(i == len(factors) - 1))
                ins.then_inc(mlp_done, 1)

        @block.scalar
        def _(act):
            def take_turned(t, i):
                act.wait_ge(turned, QUADS * t + i + 1)
                if i == 0 and not isinstance(t, int):
                    act.wait_ge(scalars_turned, QUADS * t)
                    act.wait_ge(rows_stored, 16 * t)
                nc.scalar.copy(eT[:].rearrange("p (b d) -> p d b", d=D)[:, 4 * i:4 * i + 4, :],
                               turn_ps(t, i)[0:M, :].rearrange("p (d b) -> p d b", d=4)).then_inc(eT_ready, 1)

            def take_scalars(n, q):
                act.wait_ge(scalars_turned, n + 1)
                nc.scalar.copy(ec[q][:], g_ps[:, 0:JB * M].rearrange("p (j m) -> p j m", j=JB))\
                    .then_inc(ec_ready, 1)

            def take_x1(n, q):
                act.wait_ge(l1_step, GROUPS * (n + 1))
                nc.scalar.copy(x1h[q % 2][:], x1_ps[:]).then_inc(x1h_ready, 1)

            def take_high(n, q, g):
                act.wait_ge(pair_ready, GROUPS * n + g + 1)
                if g >= RING:
                    act.wait_ge(l1_step, GROUPS * n + g - RING + 1)
                elif not (isinstance(n, int) and n == 0):
                    act.wait_ge(l1_step, GROUPS * (n - 1) + max(range(g, SPLIT, RING)) + 1)
                nc.scalar.copy(pair_hi[g % RING][:], rotated[q % 2][0:GP, g, :]).then_inc(hi_ready, 1)

            def scale_chunk(t, k, u):
                a = ACT_CHUNKS[k].index(u)
                q, j = k // JB, k % JB
                act.wait_ge(ya_ready, ONE + act_chunk(t, k, a) + 1)
                if j == 0 and a == 0:
                    act.wait_ge(ec_ready, t * QUADS + q + 1)
                if a == 0:
                    act.wait_ge(folded_ready, folded_count(t * BLOCKS + k - SLOTS))
                ps = y_act[act_chunk(0, k, a) % YA]
                for i in range(MC):
                    m = u * MC + i
                    ins = nc.scalar.activation(scaled[:, k % 2, a, i * P:(i + 1) * P], ps[:, i * P:(i + 1) * P], ACT.Copy,
                                               scale=ec[q][:, j, m:m + 1])
                ins.then_inc(scaled_ready, 1)

            def take_gram(t, k):
                n = t * BLOCKS + k
                act.wait_ge(g_done, g_count(n))
                if k == 0:
                    act.wait_ge(z3_done, ONE + t)
                nc.scalar.copy(G[:, :, k * BB:(k + 1) * BB],
                               g_ps[:, 0:BB * M1].rearrange("p (b m) -> p m b", m=M1)).then_inc(g_out, 1)

            def samples(t):
                return slice(t * P, (t + 1) * P) if isinstance(t, int) else bass.ds(t * P, P)

            def take_z(t):
                act.wait_ge(g_out, ONE + (t + 1) * BLOCKS)
                nc.scalar.copy(z[1][:, samples(t)], G[:, M, :])
                act.wait_ge(z3_done, ONE + t + 1)
                nc.scalar.copy(z[2][:, samples(t)], g_ps[:, 0:P]).then_inc(z3_out, 1)

            def front(name, i, n, q, t):
                if name == "turn":
                    take_turned(t + 1, i)
                elif name == "scalars":
                    take_scalars(n, q)
                elif name == "high":
                    take_high(n, q, i)
                elif name == "x1_high":
                    take_x1(n, q)

            def blocks(t, first, end, after, ahead):
                for k in range(first, end):
                    for u in range(CHUNKS):
                        if u == G_AT + 1:
                            if k >= LAG:
                                take_gram(t, k - LAG)
                            elif after:
                                take_gram(t - 1, k - LAG + BLOCKS)
                        if u in ACT_CHUNKS[k]:
                            scale_chunk(t, k, u)
                        if after and k * CHUNKS + u == max(L3_AT):
                            take_z(t - 1)
                        for name, i, ahead_q in front_steps(k, u):
                            if ahead_q >= QUADS and not ahead:
                                continue
                            front(name, i, t * QUADS + ahead_q, ahead_q % QUADS, t)

            act.sem_inc(scaled_ready, YA)
            act.sem_inc(g_out, ONE)
            act.sem_inc(z3_out, ONE)
            for i in range(4):
                take_turned(0, i)
            take_scalars(0, 0)
            for g in range(SPLIT):
                take_high(0, 0, g)
            take_x1(0, 0)
            for g in range(SPLIT):
                if HIGH_AT[g] < 0:
                    take_high(1, 1, g)
            blocks(0, 0, HEAD, False, True)
            with act.Fori(0, TILES - 1) as t:
                blocks(t, HEAD, BLOCKS, False, True)
                blocks(t + 1, 0, HEAD, True, True)
            blocks(TILES - 1, HEAD, BLOCKS, False, False)
            for k in range(BLOCKS - LAG, BLOCKS):
                take_gram(TILES - 1, k)

            act.wait_ge(late_in, LATE)
            for source, hi in zip(operands, operands_hi):
                nc.scalar.copy(hi, source).then_inc(split_high, 1)
            act.wait_ge(z1_out, TILES * QUADS)
            for half in range(2):
                if half == 1:
                    take_z(TILES - 1)
                    act.wait_ge(z3_out, ONE + TILES)
                for i in range(3):
                    nc.scalar.copy(z_hi[half][i], z[i][:, half * QC:(half + 1) * QC]).then_inc(split_high, 1)
            for done, (half, layer, f) in enumerate(JOBS):
                act.wait_ge(mlp_done, done + 1)
                ps = mlp_banks[done % len(mlp_banks)]
                if layer == 2:
                    nc.scalar.copy(y[:, half * QC:(half + 1) * QC], ps[0:1, :]).then_inc(mlp_out, 1)
                    continue
                part = PARTS.index((half, layer, f))
                if part >= len(relu):
                    act.wait_ge(h_low, part - len(relu) + 1)
                bias = (b1s, b2s)[layer][:, f:f + 1]
                nc.scalar.activation(relu[part % len(relu)], ps[:], ACT.Relu, bias=bias).then_inc(mlp_out, 1)

        @block.vector
        def _(dve):
            def pair(t, q, g):
                if g in (0, 2):
                    loads = sum((load[1] > 1) == (g == 2) for load in LOADS)
                    dve.wait_ge(rotated_in[q % 2][g == 2], 16 * loads * (t * QUADS // 2 + q // 2 + 1))
                factor = rotated[q % 2][0:GP]
                nc.vector.tensor_tensor(factor[:, g, :], factor[:, g, :], factor[:, FIRST, :], ALU.mult).then_inc(pair_ready, 1)

            def take_low(n, q, g):
                dve.wait_ge(hi_ready, SPLIT * n + g + 1)
                nc.vector.tensor_tensor(pair_lo[g % RING][:], rotated[q % 2][0:GP, g, :],
                                        pair_hi[g % RING][:].bitcast(F32), ALU.subtract).then_inc(lo_ready, 1)

            def take_x1(n, q, cols):
                dve.wait_ge(x1h_ready, n + 1)
                nc.vector.tensor_tensor(x1l[q % 2][:], x1_ps[:], x1h[q % 2][:].bitcast(F32), ALU.subtract)\
                    .then_inc(x1l_ready, 1)
                nc.vector.tensor_reduce(z[0][:, cols], x1_ps[:].rearrange("p (b d) -> p b d", d=D), AX.X, ALU.add)\
                    .then_inc(z1_out, 1)

            def sum_chunk(t, k, u):
                c = DVE_CHUNKS[k].index(u)
                q, j = k // JB, k % JB
                dve.wait_ge(yd_ready, dve_chunk(t, k, c) + 1)
                if j == 0 and c == 0:
                    dve.wait_ge(ec_ready, t * QUADS + q + 1)
                if c == 0:
                    dve.wait_ge(folded_ready, folded_count(t * BLOCKS + k - SLOTS))
                ps = y_dve[dve_chunk(0, k, c) % YD]
                for i in range(MC):
                    m, step = u * MC + i, c * MC + i
                    into = acc[:, k % 2, step % 2, :]
                    scalar = ec[q][:, j, m:m + 1]
                    if step < 2:
                        ins = nc.vector.tensor_scalar(into, ps[:, i * P:(i + 1) * P], scalar, None, ALU.mult)
                    else:
                        dve.wait_ge(acc_step, acc_count(dve_chunk(t, k), step - 2))
                        ins = nc.vector.scalar_tensor_tensor(out=into, in0=ps[:, i * P:(i + 1) * P], scalar=scalar,
                                                             in1=into, op0=ALU.mult, op1=ALU.add)
                    ins.then_inc(acc_step, 1)

            def take_x2(t, k):
                n = t * BLOCKS + k
                dve.wait_ge(folded_ready, folded_count(n))
                dve.wait_ge(g_done, g_count(n - SLOTS))
                nc.vector.tensor_tensor(x2[k % 2][:], folded[:, k % 2, 0:P], folded[:, k % 2, P:2 * P], ALU.add)\
                    .then_inc(x2_ready, 1)

            def front(name, i, n, q, t):
                if name == "pair":
                    pair(t, q, i)
                elif name == "low":
                    take_low(n, q, i)
                elif name == "x1_low":
                    take_x1(n, q, bass.ds(n * QB, QB) if not isinstance(n, int) else slice(n * QB, (n + 1) * QB))

            def blocks(t, first, end, after, ahead):
                for k in range(first, end):
                    for u in range(CHUNKS):
                        if u == X2_AT:
                            if k >= LAG:
                                take_x2(t, k - LAG)
                            elif after:
                                take_x2(t - 1, k - LAG + BLOCKS)
                        if u in DVE_CHUNKS[k]:
                            sum_chunk(t, k, u)
                        for name, i, ahead_q in front_steps(k, u):
                            if ahead_q >= QUADS and not ahead:
                                continue
                            front(name, i, t * QUADS + ahead_q, ahead_q % QUADS, t + ahead_q // QUADS)

            dve.sem_inc(x2_ready, SLOTS)
            dve.sem_inc(acc_step, YD * MC)
            dve.wait_ge(k1_in, 16)
            nc.vector.tensor_copy(k1h[:], k1_raw).then_inc(k1_ready, 1)
            dve.wait_ge(k1_ready, 1)
            nc.vector.tensor_tensor(k1l[:], k1_raw, k1h[:].bitcast(F32), ALU.subtract)
            dve.wait_ge(k0_in, 32)
            nc.vector.tensor_tensor(k0s[0:2 * M, 0:2, :], k0s[0:2 * M, 0:2, :], k0b[0:2 * M, 0:2, :], ALU.add)
            nc.vector.tensor_tensor(k0s[:, 2:, :], k0s[:, 2:, :], k0b[:, 2:, :], ALU.add).then_inc(k0_ready, 1)
            dve.wait_ge(k0_ready, 1)
            nc.vector.tensor_copy(k0h[:], k0s[:, 0:SPLIT, :]).then_inc(k0_ready, 1)
            dve.wait_ge(k0_ready, 2)
            nc.vector.tensor_tensor(k0l[:], k0s[:, 0:SPLIT, :], k0h[:].bitcast(F32), ALU.subtract).then_inc(k0_ready, 1)
            for i in range(2):
                nc.vector.memset(ebd[i][:, :, :, 0:M].rearrange("p j b m -> p (j b) m"), 0.0)
            dve.wait_ge(pool_const, 5)
            for i in range(2):
                last = nc.vector.tensor_copy(ebd[i][:, :, :, M], mask[:].rearrange("p (a b) -> p a b", a=1)
                                             .to_broadcast([P, JB, BB]))
            last.then_inc(ebd_cleared, 1)
            pair(0, 0, 0)
            for g in range(GROUPS):
                if g < GROUPS - 1:
                    pair(0, 0, g + 1)
                if g < SPLIT:
                    take_low(0, 0, g)
            take_x1(0, 0, slice(0, QB))
            for g in range(GROUPS):
                if PAIR_AT[g] < 0:
                    pair(0, 1, g)
            for g in range(SPLIT):
                if LOW_AT[g] < 0:
                    take_low(1, 1, g)
            blocks(0, 0, HEAD, False, True)
            with dve.Fori(0, TILES - 1) as t:
                blocks(t, HEAD, BLOCKS, False, True)
                blocks(t + 1, 0, HEAD, True, True)
            blocks(TILES - 1, HEAD, BLOCKS, False, False)
            for k in range(BLOCKS - LAG, BLOCKS):
                take_x2(TILES - 1, k)

            dve.wait_ge(g_done, g_count(TILES * BLOCKS - 1))
            lows = list(zip(operands, operands_hi, operands_lo)) + [
                (z[i][:, half * QC:(half + 1) * QC], z_hi[half][i], z_lo[half][i]) for half in range(2) for i in range(3)]
            for n, (source, hi, lo) in enumerate(lows):
                dve.wait_ge(split_high, n + 1)
                nc.vector.tensor_tensor(lo, source, hi.bitcast(F32), ALU.subtract).then_inc(split_low, 1)
            for part, (half, layer, f) in enumerate(PARTS):
                dve.wait_ge(mlp_out, JOBS.index((half, layer, f)) + 1)
                full, hi = relu[part % len(relu)], h_hi[layer][f]
                if half:
                    dve.wait_ge(mlp_done, JOBS.index((0, layer + 1, hidden[layer + 1] - 1)) + 1)
                nc.vector.tensor_copy(hi, full).then_inc(h_high, 1)
                dve.wait_ge(h_high, part + 1)
                nc.vector.tensor_tensor(h_lo[layer][f], full, hi.bitcast(F32), ALU.subtract).then_inc(h_low, 1)


def kernel(**inputs):
    import numpy as np
    import concourse.bacc as bacc
    from concourse.bass_utils import run_bass_kernel_spmd

    a = {k: np.asarray(v) for k, v in inputs.items()}
    tables = [a[f"tbl_{m}"] for m in range(M)]
    k0, k1, k2 = a["L0_rec_k0"], a["L0_rec_k1"], a["L0_rec_k2"]
    m = np.arange(M)
    pair = np.array([[(m + s) % M for s in group] for group in SHIFTS])
    own = np.broadcast_to(m, pair.shape)
    k0_first = k0[:, own, pair].transpose(2, 3, 1, 0).reshape(GP, GROUPS, P)
    k0_second = k0[:, pair, own].transpose(2, 3, 1, 0).reshape(GP, GROUPS, P)
    H1, H2 = a["W_top2"].shape
    arrays = {
        "dense_t": a["dense_ctx"].T, "ids": a["ids"],
        **{f"tbl_{i}": v for i, v in enumerate(tables)},
        "w1": a["W_top1"], "b1": a["b_top1"].reshape(H1 // P, P).T, "w2": a["W_top2"],
        "b2": a["b_top2"].reshape(H2 // P, P).T, "w3": a["W_top3"].reshape(H2 // P, P).T,
        "k0_first": k0_first, "k0_second": k0_second,
        "k1_t": k1.transpose(1, 2, 0).reshape(P, M * P), "k2_t": k2.transpose(1, 2, 0).reshape(P, M * P),
    }
    arrays = {k: np.ascontiguousarray(v) for k, v in arrays.items()}
    nc = bacc.Bacc("TRN2", target_bir_lowering=False, num_devices=1)
    ap = {k: nc.dram_tensor("in_" + k, v.shape, mybir.dt.from_np(v.dtype), kind="ExternalInput").ap()
          for k, v in arrays.items()}
    B = a["ids"].shape[0]
    out = nc.dram_tensor("out_y", (1, B), F32, kind="ExternalOutput").ap()
    e_rows = nc.dram_tensor("e_rows", (B // P * 2 * M, P * D), F32, kind="Internal").ap()
    cin_tower(nc, e_rows, ap["dense_t"], ap["ids"], [ap[f"tbl_{i}"] for i in range(M)], ap["w1"], ap["b1"], ap["w2"], ap["b2"],
              ap["w3"], ap["k0_first"], ap["k0_second"], ap["k1_t"], ap["k2_t"], out)
    r = run_bass_kernel_spmd(nc, [{"in_" + k: v for k, v in arrays.items()}], core_ids=[0])
    return r.results[0]["out_y"].reshape(B, 1)
```
